# Optimizing a Trainium2 kernel written in Bass

```python
import numpy as np
import jax
import jax.numpy as jnp

def _softmax(x, axis=-1):
    return jax.nn.softmax(x, axis=axis)

def _gelu(x):
    return jax.nn.gelu(x, approximate=True)

def _silu(x):
    return jax.nn.silu(x)

def _sigmoid(x):
    return jax.nn.sigmoid(x)

def _layernorm(x, axis=-1, eps=1e-05):
    m = jnp.mean(x, axis=axis, keepdims=True)
    v = jnp.var(x, axis=axis, keepdims=True)
    return (x - m) / jnp.sqrt(v + eps)

def _scatter_add(tgt, idx, src, axis=0):
    return tgt.at[idx].add(src)

def _segment_sum(src, seg, n):
    return jax.ops.segment_sum(src, seg, n)
kernel_name = 'mk_flamingo_gated_d1_seqx_r8_988d96'

def setup_inputs(seed: int=0):
    np.random.seed(seed)
    _w = jnp.asarray

    def _rec_inputs():
        import jax
        import jax.numpy as jnp
        _rk = jax.random.key(seed)
        x = 0.000341 + 1 * jax.random.normal(jax.random.fold_in(_rk, 1), (16, 128, 256), jnp.float32)
        _lenS = 128 - jax.random.randint(jax.random.fold_in(_rk, 7), (16,), 0, max(1, 128 // 4) + 1, jnp.int32)
        _lenS2 = 128 - jax.random.randint(jax.random.fold_in(_rk, 8), (16,), 0, max(1, 128 // 4) + 1, jnp.int32)
        _ctx_2048P = jax.random.normal(jax.random.fold_in(_rk, 11), (16, 16, 256), jnp.float32)
        _ctx_2048c = jax.random.dirichlet(jax.random.fold_in(_rk, 511), 0.3 * jnp.ones((16,), jnp.float32), (16, 128))
        _ctx_2048t = jnp.einsum('bsk,bkd->bsd', _ctx_2048c, _ctx_2048P)
        _ctx_2048t = _ctx_2048t * jax.lax.rsqrt(jnp.mean(jnp.square(_ctx_2048t)) + 1e-12) * 0.953939
        ctx_2048 = -1.47943e-05 + 1.00017 * (_ctx_2048t + 0.3 * jax.random.normal(jax.random.fold_in(_rk, 611), (16, 128, 256), jnp.float32))
        _g = jax.random.normal(jax.random.fold_in(_rk, 9001), (2, 1), jnp.float32)
        _g = jnp.sign(_g) * jnp.maximum(jnp.abs(_g), 1.0) + (_g == 0) * 1.0
        g_xattn = _g[0]
        g_ffn = _g[1]
        return (x, ctx_2048, g_xattn, g_ffn)
    x, ctx_2048, g_xattn, g_ffn = _rec_inputs()

    def _L0_xattn_setup():
        import jax, jax.numpy as jnp
        import numpy as np

        def _wkv(time_decay, time_first, k, v):
            w = -jnp.exp(time_decay)
            u = time_first
            B, T, C = k.shape
            aa = jnp.zeros((B, C), dtype=k.dtype)
            bb = jnp.zeros((B, C), dtype=k.dtype)
            pp = jnp.full((B, C), -1e+38, dtype=k.dtype)

            def step(carry, kv_t):
                aa, bb, pp = carry
                kt, vt = kv_t
                ww = u + kt
                q = jnp.maximum(pp, ww)
                e1 = jnp.exp(pp - q)
                e2 = jnp.exp(ww - q)
                y_t = (e1 * aa + e2 * vt) / (e1 * bb + e2)
                ww2 = pp + w
                q2 = jnp.maximum(ww2, kt)
                e1b = jnp.exp(ww2 - q2)
                e2b = jnp.exp(kt - q2)
                new_carry = (e1b * aa + e2b * vt, e1b * bb + e2b, q2)
                return (new_carry, y_t)
            ks = jnp.transpose(k, (1, 0, 2))
            vs = jnp.transpose(v, (1, 0, 2))
            _, ys = jax.lax.scan(step, (aa, bb, pp), (ks, vs))
            return jnp.transpose(ys, (1, 0, 2))
        key = jax.random.key(seed)
        k1, k2, k3, k4 = jax.random.split(key, 4)
        B, T, C = (8, 128, 256)
        return {'batch_size': B, 'seq_len': T, 'embedding_dim': C, 'time_decay': jax.random.normal(k1, (C,), dtype=jnp.float32), 'time_first': jax.random.normal(k2, (C,), dtype=jnp.float32), 'k': jax.random.normal(k3, (B, T, C), dtype=jnp.float32), 'v': jax.random.normal(k4, (B, T, C), dtype=jnp.float32)}
    _L0_xattn_all = _L0_xattn_setup()
    _L0_xattn_in = {k: v for k, v in _L0_xattn_all.items() if k in ('time_decay', 'time_first')}
    del _L0_xattn_all

    def _L0_ffn_setup():
        import jax
        import jax.numpy as jnp
        import numpy as np
        NUM_EXPERTS = 32
        HIDDEN = 256
        INTER = 96
        TOP_K = 8
        TAU = 0.05
        BATCH, SEQ = (2, 128)
        key = jax.random.key(seed)
        k1, k2, k3, k4 = jax.random.split(key, 4)
        return {'hidden_states': jax.random.normal(k1, (BATCH, SEQ, HIDDEN), dtype=jnp.float32), 'gate_weight': jax.random.normal(k2, (NUM_EXPERTS, HIDDEN), dtype=jnp.float32) * 0.02, 'gate_up_proj': jax.random.normal(k3, (NUM_EXPERTS, 2 * INTER, HIDDEN), dtype=jnp.float32) * 0.02, 'down_proj': jax.random.normal(k4, (NUM_EXPERTS, HIDDEN, INTER), dtype=jnp.float32) * 0.02, 'layer_alpha': jnp.array(1.0, dtype=jnp.float32)}
    _L0_ffn_all = _L0_ffn_setup()
    _L0_ffn_in = {k: v for k, v in _L0_ffn_all.items() if k in ('gate_weight', 'gate_up_proj', 'down_proj', 'layer_alpha')}
    del _L0_ffn_all
    return {'x': x, 'ctx_2048': ctx_2048, 'g_xattn': g_xattn, 'g_ffn': g_ffn, 'L0_xattn_time_decay': _L0_xattn_in['time_decay'], 'L0_xattn_time_first': _L0_xattn_in['time_first'], 'L0_ffn_gate_weight': _L0_ffn_in['gate_weight'], 'L0_ffn_gate_up_proj': _L0_ffn_in['gate_up_proj'], 'L0_ffn_down_proj': _L0_ffn_in['down_proj'], 'L0_ffn_layer_alpha': _L0_ffn_in['layer_alpha']}

def reference(x, ctx_2048, g_xattn, g_ffn, L0_xattn_time_decay, L0_xattn_time_first, L0_ffn_gate_weight, L0_ffn_gate_up_proj, L0_ffn_down_proj, L0_ffn_layer_alpha):
    import jax
    import jax.numpy as jnp

    def _L0_xattn_ref(batch_size, seq_len, embedding_dim, time_decay, time_first, k, v):
        import jax, jax.numpy as jnp
        import numpy as np

        def _wkv(time_decay, time_first, k, v):
            w = -jnp.exp(time_decay)
            u = time_first
            B, T, C = k.shape
            aa = jnp.zeros((B, C), dtype=k.dtype)
            bb = jnp.zeros((B, C), dtype=k.dtype)
            pp = jnp.full((B, C), -1e+38, dtype=k.dtype)

            def step(carry, kv_t):
                aa, bb, pp = carry
                kt, vt = kv_t
                ww = u + kt
                q = jnp.maximum(pp, ww)
                e1 = jnp.exp(pp - q)
                e2 = jnp.exp(ww - q)
                y_t = (e1 * aa + e2 * vt) / (e1 * bb + e2)
                ww2 = pp + w
                q2 = jnp.maximum(ww2, kt)
                e1b = jnp.exp(ww2 - q2)
                e2b = jnp.exp(kt - q2)
                new_carry = (e1b * aa + e2b * vt, e1b * bb + e2b, q2)
                return (new_carry, y_t)
            ks = jnp.transpose(k, (1, 0, 2))
            vs = jnp.transpose(v, (1, 0, 2))
            _, ys = jax.lax.scan(step, (aa, bb, pp), (ks, vs))
            return jnp.transpose(ys, (1, 0, 2))
        assert seq_len <= 128
        return _wkv(time_decay, time_first, k, v)

    def _L0_ffn_ref(hidden_states, gate_weight, gate_up_proj, down_proj, layer_alpha):
        import jax
        import jax.numpy as jnp
        import numpy as np
        NUM_EXPERTS = 32
        HIDDEN = 256
        INTER = 96
        TOP_K = 8
        TAU = 0.05
        BATCH, SEQ = (2, 128)
        B, S, H = hidden_states.shape
        x = hidden_states.reshape(-1, H)
        T = x.shape[0]
        logits = x @ gate_weight.T
        probs = jax.nn.softmax(logits.astype(jnp.float32), axis=-1).astype(logits.dtype)
        topv, topi = jax.lax.top_k(probs, TOP_K)
        topv = topv / jnp.clip(topv.sum(axis=-1, keepdims=True), 1e-12)
        scaled = topv * layer_alpha.astype(topv.dtype)
        active = scaled >= TAU
        empty = ~jnp.any(active, axis=-1)
        fallback = jnp.arange(TOP_K)[None, :] == jnp.argmax(scaled, axis=-1)[:, None]
        active = active | empty[:, None] & fallback
        routing_weights = topv * active.astype(topv.dtype)
        routing_weights = routing_weights / jnp.clip(routing_weights.sum(axis=-1, keepdims=True), 1e-12)
        combine = jnp.zeros((T, NUM_EXPERTS), dtype=x.dtype)
        combine = combine.at[jnp.arange(T)[:, None], topi].add(routing_weights)

        def expert_step(acc, xs):
            w_gu, w_d, c_e = xs
            gu = x @ w_gu.T
            g, u = jnp.split(gu, 2, axis=-1)
            h = jax.nn.silu(g) * u
            acc = acc + h @ w_d.T * c_e[:, None]
            return (acc, None)
        out, _ = jax.lax.scan(expert_step, jnp.zeros_like(x), (gate_up_proj, down_proj, combine.T))
        return out.reshape(B, S, H)
    x = x + jnp.tanh(g_xattn[0]) * _L0_xattn_ref(16, 128, 256, L0_xattn_time_decay, L0_xattn_time_first, _layernorm(x, axis=-1), ctx_2048)
    x = x + jnp.tanh(g_ffn[0]) * _L0_ffn_ref(_layernorm(x, axis=-1), L0_ffn_gate_weight, L0_ffn_gate_up_proj, L0_ffn_down_proj, L0_ffn_layer_alpha)
    return x

_drawn_inputs = setup_inputs


def setup_inputs(seed=0):
    import zlib

    import numpy as np

    out = dict(_drawn_inputs(seed))
    spreads = {}
    factors = {'L0_ffn_gate_weight': 8.0, 'L0_ffn_gate_up_proj': 8.0, 'L0_ffn_down_proj': 8.0}
    for name, (base, spread) in spreads.items():
        noise = np.random.default_rng([zlib.crc32(name.encode()), seed]).standard_normal(out[name].shape)
        drawn = base * np.exp(spread * noise) if base else spread * noise
        out[name] = jnp.asarray(drawn.astype(out[name].dtype))
    for name, factor in factors.items():
        out[name] = (out[name] * factor).astype(out[name].dtype)
    return out
```

```python
from contextlib import ExitStack

import concourse.bass as bass
from concourse import mybir

F32 = mybir.dt.float32
F16 = mybir.dt.float16
BF16 = mybir.dt.bfloat16
ALU = mybir.AluOpType
ACT = mybir.ActivationFunctionType
AX = mybir.AxisListType.X

P = 128
B, T, C = 16, 128, 256
KH = C // P
NTOK = B * T
BG = 4
GTOK = BG * T
NG = B // BG
NE, TOPK, INTER = 32, 8, 96
TAU = 0.05
NJ = NE * INTER // P
WT_COLS = 2 * KH * P + C
UPS = 6
SPG = NJ // UPS
NSTEP = NG * SPG
EPS = 1e-5
NEG = -1e38

WSCALE = 64.0
XSCALE = 256.0
GU_UNSCALE = 1.0 / (WSCALE * XSCALE)

CREDIT = 3
HEAD_LINKS, TAIL_LINKS = 14, 27


class Chain:

    def __init__(self, eng, sem, base):
        self.eng, self.sem, self.base, self.n = eng, sem, base, 0

    def link(self, ins):
        self.n += 1
        ins.then_inc(self.sem, 1)
        self.eng.wait_ge(self.sem, self.base + self.n)


def rwkv_moe_kernel(nc, x, xt, ctx, params, gate_wt, weights, out):
    with ExitStack() as st:
        def sb(name, shape, dt):
            return st.enter_context(nc.sbuf_tensor(name, shape, dt))

        def sem(name):
            return st.enter_context(nc.semaphore(name))

        w_hi = sb("w_hi", [P, NJ * WT_COLS], F16)
        w_lo = sb("w_lo", [P, NJ * WT_COLS], F16)
        w_stage = sb("w_stage", [P, 3, WT_COLS], F32)
        x_nat = sb("x_nat", [P, B, C], F32)
        xT = sb("xT", [P, KH, NTOK], F32)
        ctxT = sb("ctxT", [P, KH, NTOK], F32)
        xn_hi = sb("xn_hi", [P, KH, NTOK], F16)
        xn_lo = sb("xn_lo", [P, KH, NTOK], F16)
        combT = sb("combT", [3 * NE, NTOK], BF16)
        expert_of = sb("expert_of", [3 * NE, NE, INTER], BF16)
        hidden = sb("hidden", [P, 3, GTOK], F32)
        h_hi = sb("h_hi", [P, 3, GTOK], F16)
        h_lo = sb("h_lo", [P, 3, GTOK], F16)
        par = sb("par", [P, 8], F32)
        gate_w = sb("gate_w", [P, KH, NE], F32)
        ident = sb("ident", [P, P], F32)
        ident16 = sb("ident16", [P, P], BF16)
        zeros16 = sb("zeros16", [P, P], F16)
        ones32 = sb("ones32", [P, NE], F32)
        decay = sb("decay", [P, KH], F32)
        tg = sb("tg", [P, 4], F32)
        halfpow = sb("halfpow", [P, BG], F32)

        class Work:

            def __init__(self, nb, take, tag):
                def small(name, cols):
                    return sb(name + tag, [P, nb, cols], F32)[:]

                self.nb, self.S = nb, KH * nb
                S = self.S
                self.k, self.pp, self.dec = take([P, S, T + 1]), take([P, S, T + 1]), take([P, S, T + 1])
                self.kv, self.aa, self.bb = take([P, S, T + 1]), take([P, S, T + 1]), take([P, S, T + 1])
                self.e12 = take([P, 2 * S, T])
                self.e34 = sb(f"e34{tag}", [P, 2 * S, T + 1], F32)[:]
                self.t2 = sb(f"t2{tag}", [P, S, T], F32)[:]
                self.xn = x_nat[:, 0:BG, :] if nb == BG else sb(f"xn{tag}", [P, 1, C], F32)[:]
                self.x2 = None if nb == BG else sb(f"x2{tag}", [P, S, T], F32)[:]
                self.xf = self.e12 if nb == BG else sb(f"xf{tag}", [P, S, T], F32)[:]
                self.st, self.mv, self.ve = small("st", 6), small("mv", 2), small("ve", 1)
                self.rs, self.nt = small("rs", 1), small("nt", 1)
                self.st2, self.mv2, self.ve2 = small("st2", 6), small("mv2", 2), small("ve2", 1)
                self.rs2, self.nt2 = small("rs2", 1), small("nt2", 1)
                self.lg, self.v8, self.nmx = small("lg", NE), small("v8", 8), small("nmx", 1)
                self.E, self.e8, self.left = small("E", NE), small("e8", 8), small("left", NE)
                self.s8, self.r8, self.vn = small("s8", 1), small("r8", 1), small("vn", NE)
                self.act, self.mem, self.any = small("act", NE), small("mem", NE), small("any", 1)
                self.tgt, self.eq, self.cs = small("tgt", 1), small("eq", NE), small("cs", NE)
                self.wg, self.ws, self.rw = small("wg", NE), small("ws", 1), small("rw", 1)
                self.c, self.res = small("c", NE), small("res", NE)
                self.c3 = sb(f"c3{tag}", [P, nb, 3, NE], BF16)[:]

        late = {0: [w_hi, NJ // 2 * WT_COLS], 1: [w_lo, NJ // 2 * WT_COLS]}

        def take_late(shape):
            n = shape[1] * shape[2]
            for key in (0, 1):
                buf, at = late[key]
                if at + 2 * n <= NJ * WT_COLS:
                    late[key][1] = at + 2 * n
                    return buf[:, at:at + 2 * n].bitcast(F32).rearrange("p (s t) -> p s t", s=shape[1])
            raise ValueError("the startup's buffers don't fit")

        counter = [0]

        def take_own(shape):
            counter[0] += 1
            return sb(f"work{counter[0]}", shape, F32)[:]

        wide = Work(BG, take_late, "_w")
        one = Work(1, take_own, "_1")

        ps_gu = st.enter_context(nc.psum_tensor("ps_gu", [P, 2, 2, GTOK], F32))
        ps_acc = st.enter_context(nc.psum_tensor("ps_acc", [P, KH, GTOK], F32))
        ps_cb = st.enter_context(nc.psum_tensor("ps_cb", [P, GTOK], F32))
        ps_misc = st.enter_context(nc.psum_tensor("ps_misc", [P, GTOK], F32))
        gu_flat = ps_gu[:].rearrange("p a b n -> p (a b n)")
        wide.ps_kT = gu_flat[:, 0:KH * GTOK].rearrange("p (s t) -> p s t", t=T)
        wide.ps_nat = gu_flat[:, KH * GTOK:2 * KH * GTOK].rearrange("p (b c) -> p b c", c=C)
        wide.ps_xnT = wide.ps_kT
        wide.ps_lg = ps_cb[:, 0:BG * NE].rearrange("p (b e) -> p b e", e=NE)
        wide.ps_cT = ps_misc[:].bitcast(BF16)[0:3 * NE, 0:BG * T].rearrange("p (b t) -> p b t", t=T)
        one.ps_kT = ps_misc[:, C:2 * C].rearrange("p (s t) -> p s t", t=T)
        one.ps_nat = ps_misc[:, 0:C].rearrange("p (b c) -> p b c", c=C)
        one.ps_xnT = ps_misc[:, 0:C].rearrange("p (s t) -> p s t", t=T)
        one.ps_lg = ps_misc[:, 0:NE].rearrange("p (b e) -> p b e", e=NE)
        one.ps_cT = ps_misc[:].bitcast(BF16)[0:3 * NE, 0:T].rearrange("p (b t) -> p b t", t=T)

        x0_loaded = sem("x0_loaded")
        xrest_loaded = sem("xrest_loaded")
        w_loaded = [sem(f"w_loaded{i}") for i in range(3)]
        passed = sem("passed")
        consts_ready = sem("consts_ready")
        pool_step = sem("pool_step")
        pads_ready = sem("pads_ready")
        decay_exp = sem("decay_exp")
        wh_ready = sem("wh_ready")
        ws_ready = sem("ws_ready")
        w_ready = sem("w_ready")
        head_step = sem("head_step")
        var1_ready, rs1_ready, xn1_ready = sem("var1_ready"), sem("rs1_ready"), sem("xn1_ready")
        kT_ready, k_ready = sem("kT_ready"), sem("k_ready")
        d34_ready, d12_ready, e34_ready, e12_ready = (sem(n) for n in ("d34_ready", "d12_ready", "e34_ready", "e12_ready"))
        kv_ready, t2_ready, x2_ready = sem("kv_ready"), sem("t2_ready"), sem("x2_ready")
        x2_stored = sem("x2_stored")
        tail_step = sem("tail_step")
        nat_ready, var2_ready, rs2_ready, xn2_ready = (sem(n) for n in ("nat_ready", "var2_ready", "rs2_ready", "xn2_ready"))
        xnT_ready, xf_ready, xh_ready, xl_ready = (sem(n) for n in ("xnT_ready", "xf_ready", "xh_ready", "xl_ready"))
        lg_ready, nmx_ready, exp_ready, c3_ready = (sem(n) for n in ("lg_ready", "nmx_ready", "exp_ready", "c3_ready"))
        lg_taken = sem("lg_taken")
        cT_ready, comb_ready = sem("cT_ready"), sem("comb_ready")
        gu_done = sem("gu_done")
        cb_done = sem("cb_done")
        silu_ready = sem("silu_ready")
        prod_ready = sem("prod_ready")
        h_ready = sem("h_ready")
        hh_ready = sem("hh_ready")
        hl_ready = sem("hl_ready")
        down_done = sem("down_done")
        evac_ready = sem("evac_ready")
        out_done = sem("out_done")

        block = st.enter_context(nc.Block())


        def lone_wait(eng):
            eng.sem_inc(passed, 1)

        @block.sync
        def _(sp):
            for j in range(NJ):
                if j >= 3:
                    sp.wait_ge(w_ready, j - 2)
                sp.dma_start(w_stage[:, j % 3, :], weights[j]).then_inc(w_loaded[j % 3], 16)
                if j == 2:
                    for g in range(1, NG):
                        sp.dma_start(x_nat[:, BG * g:BG * g + BG, :],
                                     x[BG * g:BG * g + BG].rearrange("b t c -> t b c")).then_inc(xrest_loaded, 16)
                        sp.dma_start(xT[:, :, bass.ts(g, GTOK)], xt[g]).then_inc(xrest_loaded, 16)
                        sp.dma_start(ctxT[:, :, bass.ts(g, GTOK)], ctx[g]).then_inc(xrest_loaded, 16)
            for g in range(NG):
                sp.wait_ge(evac_ready, g + 1)
                sp.dma_start(out[g], xT[:, :, bass.ts(g, GTOK)]).then_inc(out_done, 16)
            sp.wait_ge(out_done, 16 * NG)

        def weight_high(act, j, slot, arrivals):
            act.wait_ge(w_loaded[slot], 16 * arrivals)
            nc.scalar.activation(w_hi[:, bass.ds(j * WT_COLS, WT_COLS)], w_stage[:, slot, :], ACT.Copy,
                                 scale=WSCALE).then_inc(wh_ready, 1)

        def head_act_k(act, w, ci):
            act.wait_ge(kT_ready, ci + 1)
            act.wait_ge(d34_ready, ci)
            nc.scalar.copy(w.k[:, :, 1:], w.ps_kT).then_inc(k_ready, 1)

        def head_act_exp(act, w, ci):
            act.wait_ge(d34_ready, ci + 1)
            nc.scalar.activation(w.e34[:, :, 1:], w.e34[:, :, 1:], ACT.Exp).then_inc(e34_ready, 1)
            act.wait_ge(d12_ready, ci + 1)
            nc.scalar.activation(w.e12, w.e12, ACT.Exp).then_inc(e12_ready, 1)

        def tail_act_x(act, w, b, ci):
            act.wait_ge(xnT_ready, ci + 1)
            act.wait_ge(xl_ready, ci)
            nc.scalar.activation(w.xf[:, 0:w.S, :], w.ps_xnT, ACT.Copy, scale=XSCALE).then_inc(xf_ready, 1)
            act.wait_ge(xf_ready, ci + 1)
            for kh in range(KH):
                last = nc.scalar.copy(xn_hi[:, kh, bass.ds(b * T, w.nb * T)],
                                      w.xf[:, kh * w.nb:(kh + 1) * w.nb, :].rearrange("p s t -> p (s t)"))
            last.then_inc(xh_ready, 1)

        def tail_act_exp(act, w, ci):
            act.wait_ge(nmx_ready, ci + 1)
            for i in range(w.nb):
                last = nc.scalar.activation(w.E[:, i, :], w.lg[:, i, :], ACT.Exp, bias=w.nmx[:, i, :])
            last.then_inc(exp_ready, 1)

        def tail_act_comb(act, w, b, ci):
            act.wait_ge(cT_ready, ci + 1)
            nc.scalar.copy(combT[:, bass.ds(b * T, w.nb * T)], w.ps_cT.rearrange("p b t -> p (b t)")).then_inc(comb_ready, 1)

        def unit_act_silu(act, n, s):
            act.wait_ge(gu_done, n + 1)
            act.wait_ge(hl_ready, n - 2 + CREDIT)
            nc.scalar.activation(hidden[:, s % 3, :], ps_gu[:, s % 2, 0, :], ACT.Silu,
                                 scale=GU_UNSCALE).then_inc(silu_ready, 1)

        def unit_act_high(act, n, s):
            act.wait_ge(h_ready, n + 1 + CREDIT)
            act.wait_ge(down_done, n - 2 + CREDIT)
            nc.scalar.copy(h_hi[:, s % 3, :], hidden[:, s % 3, :]).then_inc(hh_ready, 1)

        @block.scalar
        def _(act):
            act.dma_start(par[:], params).then_inc(x0_loaded, 16)
            act.dma_start(x_nat[:, 0:BG, :], x[0:BG].rearrange("b t c -> t b c")).then_inc(x0_loaded, 16)
            act.dma_start(xT[:, :, 0:GTOK], xt[0]).then_inc(x0_loaded, 16)
            act.dma_start(ctxT[:, :, 0:GTOK], ctx[0]).then_inc(x0_loaded, 16)
            act.dma_start(gate_w[:], gate_wt).then_inc(x0_loaded, 16)
            act.wait_ge(x0_loaded, 5 * 16)
            nc.scalar.activation(decay[:], par[:, 0:2], ACT.Exp)
            nc.scalar.activation(tg[:, 0:2], par[:, 4:6], ACT.Tanh).then_inc(decay_exp, 1)
            for j in range(3):
                weight_high(act, j, j % 3, j // 3 + 1)
            head_act_k(act, wide, 0)
            head_act_exp(act, wide, 0)
            for j in range(3, UPS):
                weight_high(act, j, j % 3, j // 3 + 1)
            tail_act_x(act, wide, 0, 0)
            tail_act_exp(act, wide, 0)
            tail_act_comb(act, wide, 0, 0)
            head_act_k(act, one, 1)
            head_act_exp(act, one, 1)

            def step(t, prep, tail, head):
                b = t + BG
                ci = t + 1
                for s in range(UPS):
                    n = UPS * t + s
                    unit_act_silu(act, n, s)
                    if prep:
                        weight_high(act, (t + 1) * UPS + s, s % 3, (t + 1) * 2 + s // 3 + 1)
                    unit_act_high(act, n, s)
                    if tail and s == 1:
                        tail_act_x(act, one, b, ci)
                    if tail and s == 2:
                        tail_act_exp(act, one, ci)
                    if head and s == 3:
                        head_act_k(act, one, ci + 1)
                    if head and s == 4:
                        head_act_exp(act, one, ci + 1)
                    if tail and s == 3:
                        tail_act_comb(act, one, b, ci)

            with act.Fori(0, SPG - 1) as t:
                step(t, True, True, True)
            with act.Fori(SPG - 1, NSTEP - SPG - 1) as t:
                step(t, False, True, True)
            step(NSTEP - SPG - 1, False, True, False)
            with act.Fori(NSTEP - SPG, NSTEP) as t:
                step(t, False, False, False)

        def weight_low(pool, j, slot, arrivals):
            pool.wait_ge(w_loaded[slot], 16 * arrivals)
            pool.wait_ge(wh_ready, j + 1)
            lone_wait(pool)
            nc.gpsimd.tensor_scalar(w_stage[:, slot, :], w_stage[:, slot, :], WSCALE, None, ALU.mult).then_inc(ws_ready, 1)
            pool.wait_ge(ws_ready, j + 1)
            lone_wait(pool)
            col = bass.ds(j * WT_COLS, WT_COLS)
            nc.gpsimd.tensor_tensor(w_lo[:, col], w_stage[:, slot, :], w_hi[:, col], ALU.subtract).then_inc(w_ready, 1)

        def rsqrt_pool(pool, ve, rs, ready, done, ci):
            pool.wait_ge(ready, ci + 1)
            nc.gpsimd.tensor_tensor(rs, ve, halfpow[:, 0:ve.shape[1]].unsqueeze(2), ALU.pow).then_inc(done, 1)

        def head_pool_v(pool, w, b, ci):
            S = w.S
            v = ctxT[:, :, bass.ds(b * T, w.nb * T)]
            pool.wait_ge(e34_ready, ci + 1)
            lone_wait(pool)
            for kh in range(KH):
                vk = v[:, kh, :].rearrange("p (s t) -> p s t", t=T)
                seg = slice(kh * w.nb, (kh + 1) * w.nb)
                last = nc.gpsimd.tensor_tensor(w.kv[:, seg, 1:], w.e34[:, S + seg.start:S + seg.stop, 1:], vk, ALU.mult)
            last.then_inc(kv_ready, 1)
            pool.wait_ge(e12_ready, ci + 1)
            lone_wait(pool)
            for kh in range(KH):
                vk = v[:, kh, :].rearrange("p (s t) -> p s t", t=T)
                seg = slice(kh * w.nb, (kh + 1) * w.nb)
                last = nc.gpsimd.tensor_tensor(w.t2[:, seg, :], w.e12[:, S + seg.start:S + seg.stop, :], vk, ALU.mult)
            last.then_inc(t2_ready, 1)

        def head_pool_store(pool, w, b, ci):
            pool.wait_ge(x2_ready, ci + 1)
            lone_wait(pool)
            nc.gpsimd.tensor_copy(xT[:, :, bass.ds(b * T, T)], w.x2).then_inc(x2_stored, 1)

        def tail_pool_x(pool, w, b, ci):
            pool.wait_ge(xh_ready, ci + 1)
            lone_wait(pool)
            for kh in range(KH):
                col = bass.ds(b * T, w.nb * T)
                last = nc.gpsimd.tensor_tensor(xn_lo[:, kh, col],
                                               w.xf[:, kh * w.nb:(kh + 1) * w.nb, :].rearrange("p s t -> p (s t)"),
                                               xn_hi[:, kh, col], ALU.subtract)
            last.then_inc(xl_ready, 1)

        def unit_pool_low(pool, n, s):
            pool.wait_ge(hh_ready, n + 1)
            nc.gpsimd.tensor_tensor(h_lo[:, s % 3, :], hidden[:, s % 3, :], h_hi[:, s % 3, :],
                                    ALU.subtract).then_inc(hl_ready, 1)

        @block.gpsimd
        def _(pool):
            pool.sem_inc(hl_ready, CREDIT)
            nc.gpsimd.memset(halfpow[:], -0.5)
            nc.gpsimd.memset(ident[:], 0.0)
            nc.gpsimd.memset(ident16[:], 0.0)
            nc.gpsimd.memset(zeros16[:], 0.0)
            nc.gpsimd.memset(ones32[:], 1.0)
            nc.gpsimd.memset(expert_of[:], 0.0).then_inc(pool_step, 1)
            pool.wait_ge(pool_step, 1)
            for m in (ident, ident16):
                last = nc.gpsimd.affine_select(out=m[:], in_=m[:], compare_op=ALU.not_equal, fill=1.0, base=0,
                                               pattern=[[-1, P]], channel_multiplier=1)
            last.then_inc(consts_ready, 1)
            for part in range(3):
                nc.gpsimd.affine_select(out=expert_of[:], in_=expert_of[:], compare_op=ALU.not_equal,
                                        fill=GU_UNSCALE, base=-part * NE, pattern=[[-1, NE], [0, INTER]],
                                        channel_multiplier=1).then_inc(pool_step, 1)
                pool.wait_ge(pool_step, part + 2)
            pool.sem_inc(consts_ready, 1)
            rsqrt_pool(pool, wide.ve, wide.rs, var1_ready, rs1_ready, 0)
            for j in range(3):
                weight_low(pool, j, j % 3, j // 3 + 1)
            head_pool_v(pool, wide, 0, 0)
            rsqrt_pool(pool, wide.ve2, wide.rs2, var2_ready, rs2_ready, 0)
            for j in range(3, UPS):
                weight_low(pool, j, j % 3, j // 3 + 1)
            tail_pool_x(pool, wide, 0, 0)
            rsqrt_pool(pool, one.ve, one.rs, var1_ready, rs1_ready, 1)
            head_pool_v(pool, one, BG, 1)

            def step(t, prep, tail, head):
                b = t + BG
                ci = t + 1
                for s in range(UPS):
                    n = UPS * t + s
                    unit_pool_low(pool, n, s)
                    if prep:
                        weight_low(pool, (t + 1) * UPS + s, s % 3, (t + 1) * 2 + s // 3 + 1)
                    if tail and s == 0:
                        head_pool_store(pool, one, b, ci)
                        rsqrt_pool(pool, one.ve2, one.rs2, var2_ready, rs2_ready, ci)
                    if tail and s == 1:
                        tail_pool_x(pool, one, b, ci)
                    if head and s == 1:
                        rsqrt_pool(pool, one.ve, one.rs, var1_ready, rs1_ready, ci + 1)
                    if head and s == 4:
                        head_pool_v(pool, one, b + 1, ci + 1)

            with pool.Fori(0, SPG - 1) as t:
                step(t, True, True, True)
            with pool.Fori(SPG - 1, NSTEP - SPG - 1) as t:
                step(t, False, True, True)
            step(NSTEP - SPG - 1, False, True, False)
            with pool.Fori(NSTEP - SPG, NSTEP) as t:
                step(t, False, False, False)

        def stats(ch, src, w, st_, mv, ve, ready):
            for i in range(w.nb):
                last = nc.vector.bn_stats(st_[:, i, :], src(i))
            ch.link(last)
            lone_wait(ch.eng)
            for i in range(w.nb):
                last = nc.vector.bn_aggr(mv[:, i, :], st_[:, i, :])
            ch.link(last)
            nc.vector.tensor_scalar(ve, mv[:, :, 1:2], EPS, None, ALU.add).then_inc(ready, 1)

        def normalise(dve, ch, src, dst, w, mv, ve, rs, nt, pooled, ci, done):
            dve.wait_ge(pooled, ci + 1)
            ch.link(nc.vector.tensor_tensor(nt, ve, rs, ALU.mult))
            ch.link(nc.vector.tensor_tensor(nt, nt, rs, ALU.mult))
            ch.link(nc.vector.tensor_scalar(nt, nt, -0.5, 1.5, ALU.mult, ALU.add))
            ch.link(nc.vector.tensor_tensor(rs, nt, rs, ALU.mult))
            for i in range(w.nb):
                last = nc.vector.tensor_scalar(dst(i), src(i), mv[:, i, 0:1], rs[:, i, :], ALU.subtract, ALU.mult)
            last.then_inc(done, 1)

        def head_chain(dve, ci):
            return Chain(dve, head_step, HEAD_LINKS * ci)

        def tail_chain(dve, ci):
            return Chain(dve, tail_step, TAIL_LINKS * ci)

        def head_dve_stats(dve, ch, w, b, ci):
            stats(ch, lambda i: x_nat[:, b + i, :] if isinstance(b, int) else x_nat[:, bass.ds(b, 1), :].rearrange("p a c -> p (a c)"),
                  w, w.st, w.mv, w.ve, var1_ready)

        def head_dve_norm(dve, ch, w, b, ci):
            dve.wait_ge(kT_ready, ci)
            normalise(dve, ch, lambda i: x_nat[:, b + i, :] if isinstance(b, int) else x_nat[:, bass.ds(b, 1), :].rearrange("p a c -> p (a c)"),
                      lambda i: w.xn[:, i, :], w, w.mv, w.ve, w.rs, w.nt, rs1_ready, ci, xn1_ready)

        def head_dve_max(dve, ch, w, ci):
            S, nb = w.S, w.nb
            dve.wait_ge(k_ready, ci + 1)
            ch.link(nc.vector.tensor_tensor_scan(w.pp.rearrange("p s t -> p (s t)"), w.dec.rearrange("p s t -> p (s t)"),
                                                 w.k.rearrange("p s t -> p (s t)"), NEG, ALU.add, ALU.max))
            key, before, after = w.k[:, :, 1:], w.pp[:, :, 0:T], w.pp[:, :, 1:]
            dve.wait_ge(e12_ready, ci)
            for kh in range(KH):
                seg = slice(kh * nb, (kh + 1) * nb)
                nc.vector.scalar_tensor_tensor(w.e34[:, seg, 1:], before[:, seg, :], decay[:, kh:kh + 1],
                                               after[:, seg, :], ALU.add, ALU.subtract)
            nc.vector.tensor_tensor(w.e34[:, S:, 1:], key, after, ALU.subtract).then_inc(d34_ready, 1)
            for kh in range(KH):
                seg = slice(kh * nb, (kh + 1) * nb)
                last = nc.vector.scalar_tensor_tensor(w.e12[:, S + seg.start:S + seg.stop, :], key[:, seg, :],
                                                      par[:, 2 + kh:3 + kh], before[:, seg, :], ALU.add, ALU.subtract)
            ch.link(last)
            ch.link(nc.vector.tensor_scalar(w.e12[:, 0:S, :], w.e12[:, S:, :], -1.0, 0.0, ALU.mult, ALU.min))
            nc.vector.tensor_scalar(w.e12[:, S:, :], w.e12[:, S:, :], 0.0, None, ALU.min).then_inc(d12_ready, 1)

        def head_dve_scan(dve, ch, w, ci):
            flat = lambda a: a.rearrange("p s t -> p (s t)")
            dve.wait_ge(e34_ready, ci + 1)
            nc.vector.tensor_tensor_scan(flat(w.bb), flat(w.e34[:, 0:w.S, :]), flat(w.e34[:, w.S:, :]), 0.0,
                                         ALU.mult, ALU.add)
            dve.wait_ge(kv_ready, ci + 1)
            ch.link(nc.vector.tensor_tensor_scan(flat(w.aa), flat(w.e34[:, 0:w.S, :]), flat(w.kv), 0.0,
                                                 ALU.mult, ALU.add))

        def head_dve_out(dve, ch, w, b, ci):
            dve.wait_ge(e12_ready, ci + 1)
            S = w.S
            e1, e2 = w.e12[:, 0:S, :], w.e12[:, S:, :]
            den, num = w.bb[:, :, 0:T], w.aa[:, :, 0:T]
            nc.vector.tensor_tensor(den, den, e1, ALU.mult)
            ch.link(nc.vector.tensor_tensor(num, num, e1, ALU.mult))
            nc.vector.tensor_tensor(den, den, e2, ALU.add)
            dve.wait_ge(t2_ready, ci + 1)
            ch.link(nc.vector.tensor_tensor(num, num, w.t2, ALU.add))
            ch.link(nc.vector.reciprocal(den, den))
            ch.link(nc.vector.tensor_tensor(num, num, den, ALU.mult))
            if w.x2 is not None:
                dve.wait_ge(nat_ready, ci)
                dve.wait_ge(x2_stored, ci - 1)
            for kh in range(KH):
                v = xT[:, kh, bass.ds(b * T, w.nb * T)].rearrange("p (s t) -> p s t", t=T)
                dst = v if w.x2 is None else w.x2[:, kh * w.nb:(kh + 1) * w.nb, :]
                last = nc.vector.scalar_tensor_tensor(dst, num[:, kh * w.nb:(kh + 1) * w.nb, :], tg[:, 0:1], v,
                                                      ALU.mult, ALU.add)
            last.then_inc(x2_ready, 1)
            assert ch.n <= HEAD_LINKS, ch.n
            if ch.n < HEAD_LINKS:
                dve.sem_inc(head_step, HEAD_LINKS - ch.n)

        def tail_dve_stats(dve, ch, w, ci):
            dve.wait_ge(nat_ready, ci + 1)
            stats(ch, lambda i: w.ps_nat[:, i, :], w, w.st2, w.mv2, w.ve2, var2_ready)

        def tail_dve_norm(dve, ch, w, ci):
            dve.wait_ge(xnT_ready, ci)
            dst = (lambda i: w.t2.rearrange("p s t -> p (s t)")[:, i * C:(i + 1) * C])
            normalise(dve, ch, lambda i: w.ps_nat[:, i, :], dst, w, w.mv2, w.ve2, w.rs2, w.nt2, rs2_ready, ci, xn2_ready)

        def tail_dve_logits(dve, ch, w, ci):
            dve.wait_ge(lg_ready, ci + 1)
            nc.vector.tensor_scalar(w.lg, w.ps_lg, 1.0 / XSCALE, None, ALU.mult).then_inc(lg_taken, 1)
            dve.wait_ge(lg_taken, ci + 1)
            lone_wait(dve)
            for i in range(w.nb):
                last = nc.vector.max(w.v8[:, i, :], w.lg[:, i, :])
            ch.link(last)
            nc.vector.tensor_scalar(w.nmx, w.v8[:, :, 0:1], -1.0, None, ALU.mult).then_inc(nmx_ready, 1)

        def tail_dve_route(dve, ch, w, ci):
            nbs = range(w.nb)
            dve.wait_ge(exp_ready, ci + 1)
            lone_wait(dve)
            for i in nbs:
                last = nc.vector.max(w.e8[:, i, :], w.E[:, i, :])
            ch.link(last)
            lone_wait(dve)
            for i in nbs:
                last = nc.vector.match_replace(w.left[:, i, :], w.e8[:, i, :], w.E[:, i, :], -1.0)
            nc.vector.reduce_sum(w.s8, w.e8, AX)
            ch.link(nc.vector.tensor_scalar(w.tgt, w.e8[:, :, 0:1], tg[:, 2:3], None, ALU.mult))
            nc.vector.tensor_scalar(w.mem, w.left, 0.0, None, ALU.is_lt)
            ch.link(nc.vector.scalar_tensor_tensor(w.tgt, w.e8[:, :, 7:8], tg[:, 3:4], w.tgt, ALU.mult, ALU.add))
            ch.link(nc.vector.reciprocal(w.r8, w.s8))
            for i in nbs:
                last = nc.vector.tensor_scalar(w.vn[:, i, :], w.E[:, i, :], w.r8[:, i, :], None, ALU.mult)
            ch.link(last)
            ch.link(nc.vector.tensor_scalar(w.act, w.vn, par[:, 6:7], TAU, ALU.mult, ALU.is_ge))
            nc.vector.tensor_tensor(w.act, w.act, w.mem, ALU.mult)
            for i in nbs:
                last = nc.vector.scalar_tensor_tensor(w.eq[:, i, :], w.E[:, i, :], w.tgt[:, i, :], w.mem[:, i, :],
                                                      ALU.is_equal, ALU.mult)
            ch.link(last)
            nc.vector.reduce_max(w.any, w.act, AX)
            for i in nbs:
                last = nc.vector.tensor_tensor_scan(w.cs[:, i, :], ones32[:], w.eq[:, i, :], 0.0, ALU.mult, ALU.add)
            ch.link(last)
            ch.link(nc.vector.scalar_tensor_tensor(w.eq, w.cs, 1.0, w.eq, ALU.is_equal, ALU.mult))
            ch.link(nc.vector.tensor_scalar(w.any, w.any, -1.0, 1.0, ALU.mult, ALU.add))
            for i in nbs:
                last = nc.vector.scalar_tensor_tensor(w.act[:, i, :], w.eq[:, i, :], w.any[:, i, :], w.act[:, i, :],
                                                      ALU.mult, ALU.max)
            ch.link(last)
            ch.link(nc.vector.tensor_tensor(w.wg, w.vn, w.act, ALU.mult))
            ch.link(nc.vector.reduce_sum(w.ws, w.wg, AX))
            ch.link(nc.vector.tensor_scalar(w.ws, w.ws, 1e-12, None, ALU.max))
            ch.link(nc.vector.reciprocal(w.rw, w.ws))
            for i in nbs:
                last = nc.vector.tensor_scalar(w.c[:, i, :], w.wg[:, i, :], w.rw[:, i, :], None, ALU.mult)
            ch.link(last)
            dve.wait_ge(cT_ready, ci)
            ch.link(nc.vector.tensor_copy(w.c3[:, :, 0, :], w.c))
            ch.link(nc.vector.tensor_tensor(w.res, w.c, w.c3[:, :, 0, :], ALU.subtract))
            ch.link(nc.vector.tensor_copy(w.c3[:, :, 1, :], w.res))
            nc.vector.tensor_tensor(w.c3[:, :, 2, :], w.res, w.c3[:, :, 1, :], ALU.subtract).then_inc(c3_ready, 1)
            assert ch.n <= TAIL_LINKS, ch.n
            if ch.n < TAIL_LINKS:
                dve.sem_inc(tail_step, TAIL_LINKS - ch.n)

        def unit_dve(dve, n, s):
            dve.wait_ge(silu_ready, n + 1)
            nc.vector.tensor_tensor(hidden[:, s % 3, :], hidden[:, s % 3, :], ps_gu[:, s % 2, 1, :],
                                    ALU.mult).then_inc(prod_ready, 1)
            dve.wait_ge(prod_ready, n + 1 + CREDIT)
            dve.wait_ge(cb_done, n + 1)
            nc.vector.tensor_tensor(hidden[:, s % 3, :], hidden[:, s % 3, :], ps_cb[:], ALU.mult).then_inc(h_ready, 1)

        def evacuate(dve, g):
            dve.wait_ge(down_done, NJ * (g + 1) + CREDIT)
            if not (isinstance(g, int) and g == 0):
                dve.wait_ge(x2_stored, BG * g)
            for m in range(KH):
                v = xT[:, m, bass.ts(g, GTOK)]
                last = nc.vector.scalar_tensor_tensor(v, ps_acc[:, m, :], tg[:, 1:2], v, ALU.mult, ALU.add)
            last.then_inc(evac_ready, 1)

        @block.vector
        def _(dve):
            dve.sem_inc(prod_ready, CREDIT)
            dve.sem_inc(h_ready, CREDIT)
            for w in (wide, one):
                nc.vector.memset(w.k[:, :, 0:1], NEG)
                nc.vector.memset(w.kv[:, :, 0:1], 0.0)
                nc.vector.memset(w.e34[:, :, 0:1], 0.0)
            nc.vector.memset(one.dec, 0.0)
            nc.vector.memset(wide.dec, 0.0).then_inc(pads_ready, 1)
            dve.wait_ge(decay_exp, 1)
            dve.wait_ge(pads_ready, 1)
            nc.vector.tensor_scalar(tg[:, 1:2], tg[:, 1:2], 1.0 / WSCALE, None, ALU.mult)
            nc.vector.tensor_scalar(tg[:, 2:3], par[:, 6:7], 0.0, None, ALU.is_ge)
            nc.vector.tensor_scalar(tg[:, 3:4], par[:, 6:7], 0.0, None, ALU.is_lt)
            nc.vector.tensor_scalar(decay[:], decay[:], -1.0, None, ALU.mult).then_inc(pads_ready, 1)
            dve.wait_ge(pads_ready, 2)
            for w in (wide, one):
                for kh in range(KH):
                    seg = w.dec[:, kh * w.nb:(kh + 1) * w.nb, :]
                    last = nc.vector.tensor_scalar(seg, seg, decay[:, kh:kh + 1], None, ALU.add)
            last.then_inc(pads_ready, 1)
            dve.wait_ge(pads_ready, 3)
            for w in (wide, one):
                last = nc.vector.memset(w.dec[:, :, 0:1], 2 * NEG)
            last.then_inc(pads_ready, 1)
            dve.wait_ge(pads_ready, 4)

            ch = head_chain(dve, 0)
            head_dve_stats(dve, ch, wide, 0, 0)
            head_dve_norm(dve, ch, wide, 0, 0)
            head_dve_max(dve, ch, wide, 0)
            head_dve_scan(dve, ch, wide, 0)
            head_dve_out(dve, ch, wide, 0, 0)
            ct = tail_chain(dve, 0)
            tail_dve_stats(dve, ct, wide, 0)
            dve.wait_ge(xrest_loaded, 9 * 16)
            ch = head_chain(dve, 1)
            head_dve_stats(dve, ch, one, BG, 1)
            tail_dve_norm(dve, ct, wide, 0)
            tail_dve_logits(dve, ct, wide, 0)
            tail_dve_route(dve, ct, wide, 0)
            head_dve_norm(dve, ch, one, BG, 1)
            head_dve_max(dve, ch, one, 1)
            head_dve_scan(dve, ch, one, 1)
            head_dve_out(dve, ch, one, BG, 1)

            def step(t, evac, tail, head):
                b = t + BG
                ci = t + 1
                ct, ch = tail_chain(dve, ci), head_chain(dve, ci + 1)
                for s in range(UPS):
                    unit_dve(dve, UPS * t + s, s)
                    if evac and s == 0:
                        evacuate(dve, t // SPG - 1)
                    if tail and s == 0:
                        tail_dve_stats(dve, ct, one, ci)
                    if head and s == 0:
                        head_dve_stats(dve, ch, one, b + 1, ci + 1)
                    if tail and s == 1:
                        tail_dve_norm(dve, ct, one, ci)
                    if head and s == 1:
                        head_dve_norm(dve, ch, one, b + 1, ci + 1)
                    if tail and s == 2:
                        tail_dve_logits(dve, ct, one, ci)
                    if head and s == 3:
                        head_dve_max(dve, ch, one, ci + 1)
                    if tail and s == 3:
                        tail_dve_route(dve, ct, one, ci)
                    if head and s == 4:
                        head_dve_scan(dve, ch, one, ci + 1)
                    if head and s == 5:
                        head_dve_out(dve, ch, one, b + 1, ci + 1)

            for g in range(NG - 1):
                step(SPG * g, g > 0, True, True)
                last_full = SPG * g + SPG - (g == NG - 2)
                with dve.Fori(SPG * g + 1, last_full) as t:
                    step(t, False, True, True)
            step(NSTEP - SPG - 1, False, True, False)
            step(NSTEP - SPG, True, False, False)
            with dve.Fori(NSTEP - SPG + 1, NSTEP) as t:
                step(t, False, False, False)
            evacuate(dve, NG - 1)

        def head_pe_keys(pe, w, ci):
            pe.wait_ge(xn1_ready, ci + 1)
            pe.wait_ge(lg_taken, ci)
            pe.wait_ge(k_ready, ci)
            for i in range(w.nb):
                for kh in range(KH):
                    last = nc.tensor.transpose(w.ps_kT[:, kh * w.nb + i, :], w.xn[:, i, kh * P:(kh + 1) * P], ident[:])
            last.then_inc(kT_ready, 1)

        def tail_pe_natural(pe, w, b, ci):
            pe.wait_ge(x2_ready, ci + 1)
            pe.wait_ge(comb_ready, ci)
            for i in range(w.nb):
                for kh in range(KH):
                    src = xT[:, kh, (b + i) * T:(b + i + 1) * T] if w.x2 is None else w.x2[:, kh, :]
                    last = nc.tensor.transpose(w.ps_nat[:, i, kh * P:(kh + 1) * P], src, ident[:])
            last.then_inc(nat_ready, 1)

        def tail_pe_normalised(pe, w, ci):
            pe.wait_ge(xn2_ready, ci + 1)
            nat = w.t2.rearrange("p s t -> p (s t)")
            for i in range(w.nb):
                for kh in range(KH):
                    last = nc.tensor.transpose(w.ps_xnT[:, kh * w.nb + i, :],
                                               nat[:, i * C + kh * P:i * C + (kh + 1) * P], ident[:])
            last.then_inc(xnT_ready, 1)

        def tail_pe_logits(pe, w, ci):
            pe.wait_ge(xf_ready, ci + 1)
            for i in range(w.nb):
                for kh in range(KH):
                    last = nc.tensor.matmul(w.ps_lg[:, i, :], w.xf[:, kh * w.nb + i, :], gate_w[:, kh, :],
                                            start=(kh == 0), stop=(kh == KH - 1))
            last.then_inc(lg_ready, 1)

        def tail_pe_comb(pe, w, ci, keys):
            pe.wait_ge(c3_ready, ci + 1)
            if keys:
                pe.wait_ge(k_ready, ci + 2)
            for i in range(w.nb):
                last = nc.tensor.transpose(w.ps_cT[:, i, :], w.c3[:, i, :, :].rearrange("p a e -> p (a e)"), ident16[:])
            last.then_inc(cT_ready, 1)

        def gate_up(pe, n, par_, j, g):
            pe.wait_ge(prod_ready, n - 1 + CREDIT)
            for gu in range(2):
                for kh in range(KH):
                    col = bass.ds(j * WT_COLS + (kh * 2 + gu) * P, P)
                    tok = bass.ds(g * GTOK, GTOK)
                    for i, (w, xx) in enumerate(((w_hi, xn_hi), (w_hi, xn_lo), (w_lo, xn_hi))):
                        last = nc.tensor.matmul(ps_gu[:, par_, gu, :], w[:, col], xx[:, kh, tok],
                                                start=(kh == 0 and i == 0), stop=(kh == KH - 1 and i == 2))
            last.then_inc(gu_done, 1)

        def spread(pe, n, j, g):
            pe.wait_ge(h_ready, n + CREDIT)
            nc.tensor.matmul(ps_cb[:], expert_of[:].rearrange("p e i -> p (e i)")[:, bass.ds(j * P, P)],
                             combT[:, bass.ds(g * GTOK, GTOK)], start=True, stop=True).then_inc(cb_done, 1)

        def down(pe, n, s, j, last_of_group):
            pe.wait_ge(hl_ready, n + 1 + CREDIT)
            for m in range(KH):
                col = bass.ds(j * WT_COLS + 2 * KH * P + m * P, P)
                for i, (w, h) in enumerate(((w_hi, h_hi), (w_hi, h_lo), (w_lo, h_hi))):
                    last = nc.tensor.matmul(ps_acc[:, m, :], w[:, col], h[:, s % 3, :], start=False,
                                            stop=last_of_group and i == 2, skip_group_check=True)
            last.then_inc(down_done, 1)

        def open_group(pe, g):
            if not (isinstance(g, int) and g == 0):
                pe.wait_ge(evac_ready, g)
            for m in range(KH):
                nc.tensor.matmul(ps_acc[:, m, :], zeros16[:], xn_hi[:, 0, 0:GTOK], start=True, stop=False,
                                 skip_group_check=True)

        @block.tensor
        def _(pe):
            pe.sem_inc(down_done, CREDIT)
            pe.wait_ge(consts_ready, 1)
            head_pe_keys(pe, wide, 0)
            tail_pe_natural(pe, wide, 0, 0)
            tail_pe_normalised(pe, wide, 0)
            tail_pe_logits(pe, wide, 0)
            tail_pe_comb(pe, wide, 0, False)
            pe.wait_ge(comb_ready, 1)
            head_pe_keys(pe, one, 1)
            pe.wait_ge(consts_ready, 2)
            for n in range(2):
                if n == 0:
                    pe.wait_ge(xl_ready, 1)
                    pe.wait_ge(comb_ready, 1)
                pe.wait_ge(w_ready, n + 1)
                gate_up(pe, n, n, n, 0)
                spread(pe, n, n, 0)

            def step(t, fresh, tail, head, units_left):
                b = t + BG
                ci = t + 1
                for s in range(UPS):
                    n = UPS * t + s
                    t2, s2 = (t, s + 2) if s < UPS - 2 else (t + 1, s + 2 - UPS)
                    j2 = UPS * (t2 % SPG) + s2
                    g2 = t2 // SPG
                    if s < units_left:
                        if s == UPS - 2:
                            pe.wait_ge(xl_ready, BG * g2 + 1)
                            pe.wait_ge(comb_ready, BG * g2 + 1)
                        if fresh:
                            pe.wait_ge(w_ready, n + 3)
                        gate_up(pe, n + 2, s % 2, j2, g2)
                    if tail and s == 0:
                        tail_pe_natural(pe, one, b, ci)
                    if tail and s == 1:
                        tail_pe_normalised(pe, one, ci)
                    if tail and s == 2:
                        tail_pe_logits(pe, one, ci)
                    if head and s == 2:
                        head_pe_keys(pe, one, ci + 1)
                    if tail and s == 3:
                        tail_pe_comb(pe, one, ci, head)
                    down(pe, n, s, UPS * (t % SPG) + s, s == UPS - 1)
                    if s < units_left:
                        spread(pe, n + 2, j2, g2)

            open_group(pe, 0)
            with pe.Fori(0, SPG - 1) as t:
                step(t, True, True, True, UPS)
            step(SPG - 1, False, True, True, UPS)
            for g in range(1, NG - 1):
                open_group(pe, g)
                with pe.Fori(SPG * g, SPG * (g + 1) - (g == NG - 2)) as t:
                    step(t, False, True, True, UPS)
            step(NSTEP - SPG - 1, False, True, False, UPS)
            open_group(pe, NG - 1)
            with pe.Fori(NSTEP - SPG, NSTEP - 1) as t:
                step(t, False, False, False, UPS)
            step(NSTEP - 1, False, False, False, UPS - 2)


def kernel(x, ctx_2048, g_xattn, g_ffn, L0_xattn_time_decay, L0_xattn_time_first, L0_ffn_gate_weight,
           L0_ffn_gate_up_proj, L0_ffn_down_proj, L0_ffn_layer_alpha):
    import numpy as np
    import concourse.bacc as bacc
    from concourse.bass_utils import run_bass_kernel_spmd

    def transposed(a):
        a = np.asarray(a).reshape(NG, GTOK, KH, P)
        return np.ascontiguousarray(a.transpose(0, 3, 2, 1))

    def per_channel(v):
        return np.asarray(v).reshape(KH, P).T

    def everywhere(v):
        return np.broadcast_to(np.asarray(v).reshape(1, 1), (P, 1))

    params = np.ascontiguousarray(np.concatenate(
        [per_channel(L0_xattn_time_decay), per_channel(L0_xattn_time_first), everywhere(g_xattn), everywhere(g_ffn),
         everywhere(L0_ffn_layer_alpha), everywhere(L0_ffn_layer_alpha)], axis=1))
    gate_up = np.asarray(L0_ffn_gate_up_proj).reshape(NE, 2, INTER, KH, P)
    gate_up = gate_up.transpose(1, 0, 2, 3, 4).reshape(2, NJ, P, KH, P)
    gate_up = gate_up.transpose(1, 4, 3, 0, 2).reshape(NJ, P, 2 * KH * P)
    down = np.asarray(L0_ffn_down_proj).transpose(0, 2, 1).reshape(NJ, P, C)
    weights = np.ascontiguousarray(np.concatenate([gate_up, down], axis=2))
    gate_wt = np.ascontiguousarray(np.asarray(L0_ffn_gate_weight).reshape(NE, KH, P).transpose(2, 1, 0))

    arrays = {"in_x": np.ascontiguousarray(x), "in_xt": transposed(x), "in_ctx": transposed(ctx_2048),
              "in_params": params, "in_gate": gate_wt, "in_weights": weights}
    nc = bacc.Bacc("TRN2", target_bir_lowering=False, num_devices=1)
    args = [nc.dram_tensor(name, a.shape, mybir.dt.from_np(a.dtype), kind="ExternalInput").ap()
            for name, a in arrays.items()]
    args.append(nc.dram_tensor("out_y", (NG, P, KH, GTOK), F32, kind="ExternalOutput").ap())
    rwkv_moe_kernel(nc, *args)
    r = run_bass_kernel_spmd(nc, [arrays], core_ids=[0])
    y = r.results[0]["out_y"]
    return y.transpose(0, 3, 2, 1).reshape(B, T, C)
```

```python
from contextlib import ExitStack

import concourse.bass as bass
from concourse import mybir

F32 = mybir.dt.float32
F16 = mybir.dt.float16
BF16 = mybir.dt.bfloat16
ALU = mybir.AluOpType
ACT = mybir.ActivationFunctionType
AX = mybir.AxisListType.X

P = 128
B, T, C = 16, 128, 256
KH = C // P
NTOK = B * T
BG = 4
GTOK = BG * T
NG = B // BG
NE, TOPK, INTER = 32, 8, 96
TAU = 0.05
NJ = NE * INTER // P
WT_COLS = 2 * KH * P + C
UPS = 6
SPG = NJ // UPS
NSTEP = NG * SPG
EPS = 1e-5
NEG = -1e38

WSCALE = 64.0
XSCALE = 256.0
GU_UNSCALE = 1.0 / (WSCALE * XSCALE)

CREDIT = 3
PAIR = 2
HEAD_LINKS, TAIL_LINKS = 7, 18


class Chain:

    def __init__(self, eng, sem, base):
        self.eng, self.sem, self.base, self.n = eng, sem, base, 0

    def link(self, ins):
        self.n += 1
        ins.then_inc(self.sem, 1)
        self.eng.wait_ge(self.sem, self.base + self.n)


def flat(a):
    return a.rearrange("p s t -> p (s t)")


def rwkv_moe_kernel(nc, x, xt, ctx, params, gate_wt, weights, out):
    with ExitStack() as st:
        def sb(name, shape, dt):
            return st.enter_context(nc.sbuf_tensor(name, shape, dt))

        def sem(name):
            return st.enter_context(nc.semaphore(name))

        w_hi = sb("w_hi", [P, NJ * WT_COLS], F16)
        w_lo = sb("w_lo", [P, NJ * WT_COLS], F16)
        w_stage = sb("w_stage", [P, 3, WT_COLS], F32)
        x_nat = sb("x_nat", [P, B, C], F32)
        xT = sb("xT", [P, KH, NTOK], F32)
        ctxT = sb("ctxT", [P, KH, NTOK], F32)
        xn_hi = sb("xn_hi", [P, KH, NTOK], F16)
        xn_lo = sb("xn_lo", [P, KH, NTOK], F16)
        combT = sb("combT", [2 * NE, NTOK], F16)
        expert_of = sb("expert_of", [2 * NE, NE, INTER], F16)
        hidden = sb("hidden", [P, 3, GTOK], F32)
        h_hi = sb("h_hi", [P, 3, GTOK], F16)
        h_lo = sb("h_lo", [P, 3, GTOK], F16)
        par = sb("par", [P, 8], F32)
        gate_w = sb("gate_w", [P, KH, NE], F32)
        gate_hi = sb("gate_hi", [P, KH, NE], F16)
        gate_lo = sb("gate_lo", [P, KH, NE], F16)
        ident = sb("ident", [P, P], F32)
        ident16 = sb("ident16", [P, P], F16)
        zeros16 = sb("zeros16", [P, P], F16)
        ones32 = sb("ones32", [P, NE], F32)
        decay = sb("decay", [P, KH], F32)
        tg = sb("tg", [P, 4], F32)
        halfpow = sb("halfpow", [P, BG], F32)

        class Work:

            def __init__(self, nb, first_call, b0, take, tag):
                def small(name, cols):
                    return sb(name + tag, [P, nb, cols], F32)[:]

                self.nb, self.S = nb, KH * nb
                self.first_call = first_call
                S = self.S
                self.k, self.pp, self.dec = take([P, S, T + 1]), take([P, S, T + 1]), take([P, S, T + 1])
                self.kv, self.aa, self.bb = take([P, S, T + 1]), take([P, S, T + 1]), take([P, S, T + 1])
                self.e12 = take([P, 2 * S, T])
                self.e34 = sb(f"e34{tag}", [P, 2 * S, T + 1], F32)[:]
                self.t2 = sb(f"t2{tag}", [P, S, T], F32)[:]
                self.xn = x_nat[:, b0:b0 + nb, :] if nb > 1 else sb(f"xn{tag}", [P, 1, C], F32)[:]
                self.xn2 = flat(self.t2).rearrange("p (b c) -> p b c", c=C)
                self.x2 = None if nb > 1 else sb(f"x2{tag}", [P, S, T], F32)[:]
                self.xf = self.e12 if nb > 1 else sb(f"xf{tag}", [P, S, T], F32)[:]
                self.st, self.mv, self.ve, self.rs = small("st", 6), small("mv", 2), small("ve", 1), small("rs", 1)
                self.st2, self.mv2, self.ve2, self.rs2 = small("st2", 6), small("mv2", 2), small("ve2", 1), small("rs2", 1)
                self.lg, self.v8, self.nmx = small("lg", NE), small("v8", 8), small("nmx", 1)
                self.E, self.e8, self.left = small("E", NE), small("e8", 8), small("left", NE)
                self.s8, self.r8, self.vn = small("s8", 1), small("r8", 1), small("vn", NE)
                self.act, self.any = small("act", NE), small("any", 1)
                self.tgt, self.eq, self.cs = small("tgt", 1), small("eq", NE), small("cs", NE)
                self.wg, self.ws, self.rw = small("wg", NE), small("ws", 1), small("rw", 1)
                self.c = small("c", NE)
                self.c2 = sb(f"c2{tag}", [P, nb, 2, NE], F16)[:]
                self.head_step, self.tail_step = sem(f"head_step{tag}"), sem(f"tail_step{tag}")
                self.pool_step = sem(f"pool_step{tag}")

        late = {0: [w_hi, NJ // 2 * WT_COLS], 1: [w_lo, NJ // 2 * WT_COLS]}

        def take_late(shape):
            n = shape[1] * shape[2]
            for key in (0, 1):
                buf, at = late[key]
                if at + 2 * n <= NJ * WT_COLS:
                    late[key][1] = at + 2 * n
                    return buf[:, at:at + 2 * n].bitcast(F32).rearrange("p (s t) -> p s t", s=shape[1])
            raise ValueError("the startup's buffers don't fit")

        counter = [0]

        def take_own(shape):
            counter[0] += 1
            return sb(f"work{counter[0]}", shape, F32)[:]

        pairs = [Work(PAIR, i, PAIR * i, take_late, f"_p{i}") for i in range(2)]
        one = Work(1, 2, None, take_own, "_1")

        ps_gu = st.enter_context(nc.psum_tensor("ps_gu", [P, 2, 2, GTOK], F32))
        ps_acc = st.enter_context(nc.psum_tensor("ps_acc", [P, KH, GTOK], F32))
        ps_cb = st.enter_context(nc.psum_tensor("ps_cb", [P, GTOK], F32))
        ps_misc = st.enter_context(nc.psum_tensor("ps_misc", [P, GTOK], F32))

        def psum_views(w, keys, nat, xnT, lg, cT):
            w.ps_kT = keys.rearrange("p (s t) -> p s t", t=T)
            w.ps_nat = nat.rearrange("p (b c) -> p b c", c=C)
            w.ps_xnT = xnT.rearrange("p (s t) -> p s t", t=T)
            w.ps_lg = lg.rearrange("p (b e) -> p b e", e=NE)
            w.ps_cT = cT.bitcast(F16)[0:2 * NE, 0:w.nb * T].rearrange("p (b t) -> p b t", t=T)

        psum_views(pairs[0], ps_gu[:, 0, 0, :], ps_gu[:, 0, 1, :], ps_gu[:, 0, 0, :], ps_cb[:, 0:PAIR * NE], ps_acc[:, 0, :])
        psum_views(pairs[1], ps_gu[:, 1, 0, :], ps_gu[:, 1, 1, :], ps_gu[:, 1, 0, :], ps_misc[:, 0:PAIR * NE], ps_acc[:, 1, :])
        psum_views(one, ps_misc[:, C:2 * C], ps_misc[:, 0:C], ps_misc[:, 0:C], ps_misc[:, 0:NE], ps_misc[:, :])

        par_loaded = sem("par_loaded")
        x0_loaded = [sem(f"x0_loaded{i}") for i in range(2)]
        xt0_loaded = sem("xt0_loaded")
        xrest_loaded = sem("xrest_loaded")
        w_loaded = [sem(f"w_loaded{i}") for i in range(3)]
        passed = sem("passed")
        consts_ready = sem("consts_ready")
        const_step = sem("const_step")
        setup_step = sem("setup_step")
        gates_ready = sem("gates_ready")
        gate_split = sem("gate_split")
        wh_ready = sem("wh_ready")
        w_ready = sem("w_ready")
        var1_ready = sem("var1_ready")
        rs1_ready = sem("rs1_ready")
        xn1_ready = sem("xn1_ready")
        kT_ready = sem("kT_ready")
        k_ready = sem("k_ready")
        d34_ready, d12_ready = sem("d34_ready"), sem("d12_ready")
        e34_ready, e12_ready = sem("e34_ready"), sem("e12_ready")
        kv_ready, t2_ready = sem("kv_ready"), sem("t2_ready")
        sums_ready = sem("sums_ready")
        den_ready, num_ready = sem("den_ready"), sem("num_ready")
        x2_ready = sem("x2_ready")
        x2_stored = sem("x2_stored")
        nat_ready = sem("nat_ready")
        var2_ready, rs2_ready, xn2_ready = sem("var2_ready"), sem("rs2_ready"), sem("xn2_ready")
        xnT_ready = sem("xnT_ready")
        xh_ready = sem("xh_ready")
        xf_copied = sem("xf_copied")
        xl_ready = sem("xl_ready")
        lg_ready, lg_taken = sem("lg_ready"), sem("lg_taken")
        nmx_ready = sem("nmx_ready")
        exp_ready = sem("exp_ready")
        c2_ready = sem("c2_ready")
        cT_ready, comb_ready = sem("cT_ready"), sem("comb_ready")
        gu_done = sem("gu_done")
        cb_done = sem("cb_done")
        silu_ready = sem("silu_ready")
        prod_ready = sem("prod_ready")
        h_ready = sem("h_ready")
        hh_ready = sem("hh_ready")
        hl_ready = sem("hl_ready")
        down_done = sem("down_done")
        evac_ready = sem("evac_ready")
        out_done = sem("out_done")

        block = st.enter_context(nc.Block())

        def lone_wait(eng):
            eng.sem_inc(passed, 1)

        def run_steps(eng, step):
            step(0, True, True, True, True, False)
            with eng.Fori(1, SPG - 1) as t:
                step(t, False, True, True, True, False)
            step(SPG - 1, False, False, True, True, False)
            for g in range(1, NG - 1):
                step(SPG * g, True, False, True, True, False)
                with eng.Fori(SPG * g + 1, SPG * (g + 1) - (g == NG - 2)) as t:
                    step(t, False, False, True, True, False)
            step(NSTEP - SPG - 1, False, False, True, False, False)
            step(NSTEP - SPG, True, False, False, False, False)
            with eng.Fori(NSTEP - SPG + 1, NSTEP - 1) as t:
                step(t, False, False, False, False, False)
            step(NSTEP - 1, False, False, False, False, True)


        @block.sync
        def _(sp):
            for i in range(2):
                sp.dma_start(x_nat[:, PAIR * i:PAIR * i + PAIR, :],
                             x[PAIR * i:PAIR * i + PAIR].rearrange("b t c -> t b c")).then_inc(x0_loaded[i], 16)
            for j in range(NJ):
                if j >= 3:
                    sp.wait_ge(w_ready, j - 2)
                sp.dma_start(w_stage[:, j % 3, :], weights[j]).then_inc(w_loaded[j % 3], 16)
                if j == 2:
                    sp.dma_start(x_nat[:, BG:B, :], x[BG:B].rearrange("b t c -> t b c")).then_inc(xrest_loaded, 16)
                    for g in range(1, NG):
                        sp.dma_start(xT[:, :, bass.ts(g, GTOK)], xt[g]).then_inc(xrest_loaded, 16)
                        sp.dma_start(ctxT[:, :, bass.ts(g, GTOK)], ctx[g]).then_inc(xrest_loaded, 16)
            for g in range(NG):
                sp.wait_ge(evac_ready, g + 1)
                sp.dma_start(out[g], xT[:, :, bass.ts(g, GTOK)]).then_inc(out_done, 16)
            sp.wait_ge(out_done, 16 * NG)

        def weight_high(act, j, slot, arrivals):
            act.wait_ge(w_loaded[slot], 16 * arrivals)
            stage = w_stage[:, slot, :]
            nc.scalar.activation(w_hi[:, bass.ds(j * WT_COLS, WT_COLS)], stage, ACT.Copy, scale=WSCALE)
            nc.scalar.activation(stage, stage, ACT.Copy, scale=WSCALE).then_inc(wh_ready, 1)

        def head_act_k(act, w, ci):
            act.wait_ge(kT_ready, ci + 1)
            if w.nb == 1:
                act.wait_ge(d12_ready, ci)
            nc.scalar.copy(w.k[:, :, 1:], w.ps_kT).then_inc(k_ready, 1)

        def head_act_e34(act, w, ci):
            act.wait_ge(d34_ready, ci + 1)
            nc.scalar.activation(w.e34[:, :, 1:], w.e34[:, :, 1:], ACT.Exp).then_inc(e34_ready, 1)

        def head_act_e12(act, w, ci):
            act.wait_ge(d12_ready, ci + 1)
            nc.scalar.activation(w.e12, w.e12, ACT.Exp).then_inc(e12_ready, 1)

        def head_act_store(act, w, b, ci):
            act.wait_ge(x2_ready, ci + 1)
            nc.scalar.copy(xT[:, :, bass.ds(b * T, T)], w.x2).then_inc(x2_stored, 1)

        def tail_act_x(act, w, b, ci):
            act.wait_ge(xnT_ready, ci + 1)
            if w.nb == 1:
                act.wait_ge(xl_ready, ci)
            nc.scalar.activation(w.xf[:, 0:w.S, :], w.ps_xnT, ACT.Copy, scale=XSCALE).then_inc(xf_copied, 1)
            act.wait_ge(xf_copied, ci + 1)
            nc.scalar.copy(xn_hi[:, :, bass.ds(b * T, w.nb * T)],
                           w.xf[:, 0:w.S, :].rearrange("p (k s) t -> p k (s t)", k=KH)).then_inc(xh_ready, 1)

        def tail_act_exp(act, w, ci):
            act.wait_ge(nmx_ready, ci + 1)
            for i in range(w.nb):
                last = nc.scalar.activation(w.E[:, i, :], w.lg[:, i, :], ACT.Exp, bias=w.nmx[:, i, :])
            last.then_inc(exp_ready, 1)

        def tail_act_comb(act, w, b, ci):
            act.wait_ge(cT_ready, ci + 1)
            nc.scalar.copy(combT[:, bass.ds(b * T, w.nb * T)], w.ps_cT.rearrange("p b t -> p (b t)")).then_inc(comb_ready, 1)

        def unit_act_silu(act, n, s):
            act.wait_ge(gu_done, n + 1)
            act.wait_ge(hl_ready, n - 2 + CREDIT)
            nc.scalar.activation(hidden[:, s % 3, :], ps_gu[:, s % 2, 0, :], ACT.Silu,
                                 scale=GU_UNSCALE).then_inc(silu_ready, 1)

        def unit_act_high(act, n, s):
            act.wait_ge(h_ready, n + 1 + CREDIT)
            act.wait_ge(down_done, n - 2 + CREDIT)
            nc.scalar.copy(h_hi[:, s % 3, :], hidden[:, s % 3, :]).then_inc(hh_ready, 1)

        @block.scalar
        def _(act):
            act.dma_start(par[:], params).then_inc(par_loaded, 16)
            act.dma_start(gate_w[:], gate_wt).then_inc(par_loaded, 16)
            act.dma_start(xT[:, :, 0:GTOK], xt[0]).then_inc(xt0_loaded, 16)
            act.dma_start(ctxT[:, :, 0:GTOK], ctx[0]).then_inc(xt0_loaded, 16)
            act.wait_ge(par_loaded, 2 * 16)
            nc.scalar.activation(decay[:], par[:, 0:2], ACT.Exp)
            nc.scalar.activation(tg[:, 0:2], par[:, 4:6], ACT.Tanh)
            nc.scalar.activation(gate_hi[:], gate_w[:], ACT.Copy, scale=WSCALE).then_inc(gates_ready, 1)
            for i in range(2):
                head_act_k(act, pairs[i], i)
            for i in range(2):
                head_act_e34(act, pairs[i], i)
                head_act_e12(act, pairs[i], i)
            for j in range(UPS // 2):
                weight_high(act, j, j % 3, j // 3 + 1)
            head_act_k(act, one, 2)
            for i in range(2):
                tail_act_x(act, pairs[i], PAIR * i, i)
            head_act_e34(act, one, 2)
            for i in range(2):
                tail_act_exp(act, pairs[i], i)
            head_act_e12(act, one, 2)
            for j in range(UPS // 2, UPS):
                weight_high(act, j, j % 3, j // 3 + 1)
            for i in range(2):
                tail_act_comb(act, pairs[i], PAIR * i, i)
            unit_act_silu(act, 0, 0)
            unit_act_high(act, 0, 0)
            unit_act_silu(act, 1, 1)

            def step(t, opens, prep, tail, head, ending):
                b, ci = t + BG, t + 2
                for s in range(UPS):
                    n = UPS * t + s
                    if not ending or s < UPS - 1:
                        unit_act_high(act, n + 1, s + 1)
                    if tail and s == 0:
                        head_act_store(act, one, b, ci)
                    if head and s == 1:
                        head_act_k(act, one, ci + 1)
                    if tail and s == 1:
                        tail_act_x(act, one, b, ci)
                    if head and s == 2:
                        head_act_e34(act, one, ci + 1)
                    if tail and s == 2:
                        tail_act_exp(act, one, ci)
                    if head and s == 2:
                        head_act_e12(act, one, ci + 1)
                    if prep:
                        weight_high(act, (t + 1) * UPS + s, s % 3, (t + 1) * 2 + s // 3 + 1)
                    if tail and s == 4:
                        tail_act_comb(act, one, b, ci)
                    if not ending or s < UPS - 2:
                        unit_act_silu(act, n + 2, s + 2)

            run_steps(act, step)

        def weight_low(pool, j, slot):
            pool.wait_ge(wh_ready, j + 1)
            lone_wait(pool)
            col = bass.ds(j * WT_COLS, WT_COLS)
            nc.gpsimd.tensor_tensor(w_lo[:, col], w_stage[:, slot, :], w_hi[:, col], ALU.subtract).then_inc(w_ready, 1)

        def rsqrt_pool(pool, ve, rs, ready, done, ci):
            pool.wait_ge(ready, ci + 1)
            nc.gpsimd.tensor_tensor(rs, ve, halfpow[:, 0:ve.shape[1]].unsqueeze(2), ALU.pow).then_inc(done, 1)

        def head_pool_v(pool, w, b, ci):
            S = w.S

            def by_half(a):
                return a.rearrange("p (k s) t -> p k s t", k=KH) if w.nb > 1 else a

            v = ctxT[:, :, bass.ds(b * T, w.nb * T)]
            if w.nb > 1:
                v = v.rearrange("p k (s t) -> p k s t", t=T)
                pool.wait_ge(xt0_loaded, 2 * 16)
            pool.wait_ge(e34_ready, ci + 1)
            lone_wait(pool)
            nc.gpsimd.tensor_tensor(by_half(w.kv[:, :, 1:]), by_half(w.e34[:, S:, 1:]), v, ALU.mult).then_inc(kv_ready, 1)
            pool.wait_ge(e12_ready, ci + 1)
            lone_wait(pool)
            nc.gpsimd.tensor_tensor(by_half(w.t2), by_half(w.e12[:, S:, :]), v, ALU.mult).then_inc(t2_ready, 1)

        def head_pool_fraction(pool, w, ci):
            ch = Chain(pool, w.pool_step, 2 * (ci - w.first_call))
            e1, e2 = w.e12[:, 0:w.S, :], w.e12[:, w.S:, :]
            den, num = w.bb[:, :, 0:T], w.aa[:, :, 0:T]
            pool.wait_ge(sums_ready, ci + 1)
            ch.link(nc.gpsimd.tensor_tensor(den, den, e1, ALU.mult))
            nc.gpsimd.tensor_tensor(den, den, e2, ALU.add).then_inc(den_ready, 1)
            pool.wait_ge(t2_ready, ci + 1)
            ch.link(nc.gpsimd.tensor_tensor(num, num, e1, ALU.mult))
            nc.gpsimd.tensor_tensor(num, num, w.t2, ALU.add).then_inc(num_ready, 1)

        def tail_pool_x(pool, w, b, ci):
            pool.wait_ge(xh_ready, ci + 1)
            lone_wait(pool)
            col = bass.ds(b * T, w.nb * T)
            nc.gpsimd.tensor_tensor(xn_lo[:, :, col], w.xf[:, 0:w.S, :].rearrange("p (k s) t -> p k (s t)", k=KH),
                                    xn_hi[:, :, col], ALU.subtract).then_inc(xl_ready, 1)

        def unit_pool_low(pool, n, s):
            pool.wait_ge(hh_ready, n + 1)
            nc.gpsimd.tensor_tensor(h_lo[:, s % 3, :], hidden[:, s % 3, :], h_hi[:, s % 3, :],
                                    ALU.subtract).then_inc(hl_ready, 1)

        @block.gpsimd
        def _(pool):
            pool.sem_inc(hl_ready, CREDIT)
            nc.gpsimd.memset(halfpow[:], -0.5)
            nc.gpsimd.memset(ident[:], 0.0)
            nc.gpsimd.memset(ident16[:], 0.0)
            nc.gpsimd.memset(zeros16[:], 0.0)
            nc.gpsimd.memset(ones32[:], 1.0)
            nc.gpsimd.memset(expert_of[:], 0.0).then_inc(const_step, 1)
            pool.wait_ge(const_step, 1)
            for m in (ident, ident16):
                last = nc.gpsimd.affine_select(out=m[:], in_=m[:], compare_op=ALU.not_equal, fill=1.0, base=0,
                                               pattern=[[-1, P]], channel_multiplier=1)
            last.then_inc(consts_ready, 1)
            for i in range(2):
                rsqrt_pool(pool, pairs[i].ve, pairs[i].rs, var1_ready, rs1_ready, i)
            for part in range(2):
                nc.gpsimd.affine_select(out=expert_of[:], in_=expert_of[:], compare_op=ALU.not_equal,
                                        fill=GU_UNSCALE, base=-part * NE, pattern=[[-1, NE], [0, INTER]],
                                        channel_multiplier=1).then_inc(const_step, 1)
                pool.wait_ge(const_step, part + 2)
            pool.sem_inc(consts_ready, 1)
            for i in range(2):
                head_pool_v(pool, pairs[i], PAIR * i, i)
            for i in range(2):
                head_pool_fraction(pool, pairs[i], i)
            rsqrt_pool(pool, one.ve, one.rs, var1_ready, rs1_ready, 2)
            for j in range(UPS // 2):
                weight_low(pool, j, j % 3)
            for i in range(2):
                rsqrt_pool(pool, pairs[i].ve2, pairs[i].rs2, var2_ready, rs2_ready, i)
            for i in range(2):
                tail_pool_x(pool, pairs[i], PAIR * i, i)
            head_pool_v(pool, one, BG, 2)
            for j in range(UPS // 2, UPS):
                weight_low(pool, j, j % 3)
            head_pool_fraction(pool, one, 2)
            unit_pool_low(pool, 0, 0)

            def step(t, opens, prep, tail, head, ending):
                b, ci = t + BG, t + 2
                for s in range(UPS):
                    n = UPS * t + s
                    if tail and s == 0:
                        rsqrt_pool(pool, one.ve2, one.rs2, var2_ready, rs2_ready, ci)
                    if head and s == 0:
                        rsqrt_pool(pool, one.ve, one.rs, var1_ready, rs1_ready, ci + 1)
                    if tail and s == 1:
                        tail_pool_x(pool, one, b, ci)
                    if not ending or s < UPS - 1:
                        unit_pool_low(pool, n + 1, s + 1)
                    if head and s == 3:
                        head_pool_v(pool, one, b + 1, ci + 1)
                    if head and s == 4:
                        head_pool_fraction(pool, one, ci + 1)
                    if prep:
                        weight_low(pool, (t + 1) * UPS + s, s % 3)

            run_steps(pool, step)

        def stats(ch, src, w, st_, mv, ve, ready):
            for i in range(w.nb):
                last = nc.vector.bn_stats(st_[:, i, :], src(i))
            ch.link(last)
            lone_wait(ch.eng)
            for i in range(w.nb):
                last = nc.vector.bn_aggr(mv[:, i, :], st_[:, i, :])
            ch.link(last)
            nc.vector.tensor_scalar(ve, mv[:, :, 1:2], EPS, None, ALU.add).then_inc(ready, 1)

        def normalise(dve, src, dst, w, mv, rs, pooled, ci, done):
            dve.wait_ge(pooled, ci + 1)
            for i in range(w.nb):
                last = nc.vector.tensor_scalar(dst(i), src(i), mv[:, i, 0:1], rs[:, i, :], ALU.subtract, ALU.mult)
            last.then_inc(done, 1)

        def head_chain(dve, w, ci):
            return Chain(dve, w.head_step, HEAD_LINKS * (ci - w.first_call))

        def tail_chain(dve, w, ci):
            return Chain(dve, w.tail_step, TAIL_LINKS * (ci - w.first_call))

        def tokens(b):
            return lambda i: x_nat[:, bass.ds(b + i, 1), :].rearrange("p a c -> p (a c)")

        def head_dve_stats(dve, ch, w, b, ci):
            stats(ch, tokens(b), w, w.st, w.mv, w.ve, var1_ready)

        def head_dve_norm(dve, ch, w, b, ci):
            if w.nb == 1:
                dve.wait_ge(kT_ready, ci)
            normalise(dve, tokens(b), lambda i: w.xn[:, i, :], w, w.mv, w.rs, rs1_ready, ci, xn1_ready)

        def head_dve_max(dve, ch, w, ci):
            S, nb = w.S, w.nb
            dve.wait_ge(k_ready, ci + 1)
            ch.link(nc.vector.tensor_tensor_scan(flat(w.pp), flat(w.dec), flat(w.k), NEG, ALU.add, ALU.max))
            before, after = w.pp[:, :, 0:T], w.pp[:, :, 1:]
            for kh in range(KH):
                seg = slice(kh * nb, (kh + 1) * nb)
                nc.vector.scalar_tensor_tensor(w.e34[:, seg, 1:], before[:, seg, :], decay[:, kh:kh + 1],
                                               after[:, seg, :], ALU.add, ALU.subtract)
            nc.vector.tensor_tensor(w.e34[:, S:, 1:], w.k[:, :, 1:], after, ALU.subtract).then_inc(d34_ready, 1)

        def head_dve_ends(dve, ch, w, ci):
            S, nb = w.S, w.nb
            if nb == 1:
                dve.wait_ge(num_ready, ci)
            for kh in range(KH):
                lo, hi = kh * nb, (kh + 1) * nb
                last = nc.vector.scalar_tensor_tensor(w.e12[:, S + lo:S + hi, :], w.k[:, lo:hi, 1:],
                                                      par[:, 2 + kh:3 + kh], w.pp[:, lo:hi, 0:T], ALU.add, ALU.subtract)
            ch.link(last)
            ch.link(nc.vector.tensor_scalar(w.e12[:, 0:S, :], w.e12[:, S:, :], -1.0, 0.0, ALU.mult, ALU.min))
            nc.vector.tensor_scalar(w.e12[:, S:, :], w.e12[:, S:, :], 0.0, None, ALU.min).then_inc(d12_ready, 1)

        def head_dve_sums(dve, ch, w, ci):
            e3, e4 = flat(w.e34[:, 0:w.S, :]), flat(w.e34[:, w.S:, :])
            dve.wait_ge(e34_ready, ci + 1)
            nc.vector.tensor_tensor_scan(flat(w.bb), e3, e4, 0.0, ALU.mult, ALU.add)
            dve.wait_ge(kv_ready, ci + 1)
            nc.vector.tensor_tensor_scan(flat(w.aa), e3, flat(w.kv), 0.0, ALU.mult, ALU.add).then_inc(sums_ready, 1)

        def head_dve_out(dve, ch, w, b, ci):
            den, num = w.bb[:, :, 0:T], w.aa[:, :, 0:T]
            dve.wait_ge(den_ready, ci + 1)
            ch.link(nc.vector.reciprocal(den, den))
            dve.wait_ge(num_ready, ci + 1)
            ch.link(nc.vector.scalar_tensor_tensor(num, num, tg[:, 0:1], den, ALU.mult, ALU.mult))
            v = xT[:, :, bass.ds(b * T, w.nb * T)]
            if w.nb > 1:
                dve.wait_ge(xt0_loaded, 2 * 16)
                v = v.rearrange("p k (s t) -> p k s t", t=T)
                num = num.rearrange("p (k s) t -> p k s t", k=KH)
                nc.vector.tensor_tensor(v, num, v, ALU.add).then_inc(x2_ready, 1)
            else:
                dve.wait_ge(nat_ready, ci)
                if not (isinstance(ci, int) and ci == one.first_call):
                    dve.wait_ge(x2_stored, ci - 2)
                lone_wait(dve)
                nc.vector.tensor_tensor(w.x2, num, v, ALU.add).then_inc(x2_ready, 1)
            assert ch.n == HEAD_LINKS, ch.n

        def tail_dve_stats(dve, ch, w, ci):
            dve.wait_ge(nat_ready, ci + 1)
            stats(ch, lambda i: w.ps_nat[:, i, :], w, w.st2, w.mv2, w.ve2, var2_ready)

        def tail_dve_norm(dve, ch, w, ci):
            if w.nb == 1:
                dve.wait_ge(xnT_ready, ci)
            normalise(dve, lambda i: w.ps_nat[:, i, :], lambda i: w.xn2[:, i, :], w, w.mv2, w.rs2, rs2_ready, ci, xn2_ready)

        def tail_dve_logits(dve, ch, w, ci):
            dve.wait_ge(lg_ready, ci + 1)
            nc.vector.tensor_scalar(w.lg, w.ps_lg, GU_UNSCALE, None, ALU.mult).then_inc(lg_taken, 1)
            dve.wait_ge(lg_taken, ci + 1)
            lone_wait(dve)
            for i in range(w.nb):
                last = nc.vector.max(w.v8[:, i, :], w.lg[:, i, :])
            ch.link(last)
            nc.vector.tensor_scalar(w.nmx, w.v8[:, :, 0:1], -1.0, None, ALU.mult).then_inc(nmx_ready, 1)

        def tail_dve_route(dve, ch, w, ci):
            nbs = range(w.nb)
            dve.wait_ge(exp_ready, ci + 1)
            lone_wait(dve)
            for i in nbs:
                last = nc.vector.max(w.e8[:, i, :], w.E[:, i, :])
            ch.link(last)
            ch.link(nc.vector.reduce_sum(w.s8, w.e8, AX))
            ch.link(nc.vector.tensor_scalar(w.tgt, w.e8[:, :, 0:1], tg[:, 2:3], None, ALU.mult))
            nc.vector.reciprocal(w.r8, w.s8)
            ch.link(nc.vector.scalar_tensor_tensor(w.tgt, w.e8[:, :, 7:8], tg[:, 3:4], w.tgt, ALU.mult, ALU.add))
            lone_wait(dve)
            for i in nbs:
                nc.vector.match_replace(w.left[:, i, :], w.e8[:, i, :], w.E[:, i, :], -1.0)
            for i in nbs:
                last = nc.vector.tensor_scalar(w.vn[:, i, :], w.E[:, i, :], w.r8[:, i, :], None, ALU.mult)
            ch.link(last)
            for i in nbs:
                nc.vector.tensor_scalar(w.eq[:, i, :], w.E[:, i, :], w.tgt[:, i, :], None, ALU.is_equal)
            ch.link(nc.vector.tensor_scalar(w.act, w.vn, par[:, 6:7], TAU, ALU.mult, ALU.is_ge))
            for i in nbs:
                nc.vector.tensor_tensor_scan(w.cs[:, i, :], ones32[:], w.eq[:, i, :], 0.0, ALU.mult, ALU.add)
            ch.link(nc.vector.scalar_tensor_tensor(w.act, w.left, 0.0, w.act, ALU.is_lt, ALU.mult))
            nc.vector.scalar_tensor_tensor(w.eq, w.cs, 1.0, w.eq, ALU.is_equal, ALU.mult)
            ch.link(nc.vector.reduce_max(w.any, w.act, AX))
            for i in nbs:
                last = nc.vector.scalar_tensor_tensor(w.act[:, i, :], w.eq[:, i, :], w.any[:, i, :], w.act[:, i, :],
                                                      ALU.is_gt, ALU.max)
            ch.link(last)
            ch.link(nc.vector.tensor_tensor(w.wg, w.vn, w.act, ALU.mult))
            ch.link(nc.vector.reduce_sum(w.ws, w.wg, AX))
            ch.link(nc.vector.tensor_scalar(w.ws, w.ws, 1e-12, None, ALU.max))
            ch.link(nc.vector.reciprocal(w.rw, w.ws))
            if w.nb == 1:
                dve.wait_ge(cT_ready, ci)
            for i in nbs:
                last = nc.vector.tensor_scalar(w.c[:, i, :], w.wg[:, i, :], w.rw[:, i, :], None, ALU.mult)
            ch.link(last)
            ch.link(nc.vector.tensor_copy(w.c2[:, :, 0, :], w.c))
            nc.vector.tensor_tensor(w.c2[:, :, 1, :], w.c, w.c2[:, :, 0, :], ALU.subtract).then_inc(c2_ready, 1)
            assert ch.n == TAIL_LINKS, ch.n

        def unit_dve_prod(dve, n, s):
            dve.wait_ge(silu_ready, n + 1)
            nc.vector.tensor_tensor(hidden[:, s % 3, :], hidden[:, s % 3, :], ps_gu[:, s % 2, 1, :],
                                    ALU.mult).then_inc(prod_ready, 1)

        def unit_dve_h(dve, n, s):
            dve.wait_ge(prod_ready, n + 1 + CREDIT)
            dve.wait_ge(cb_done, n + 1)
            nc.vector.tensor_tensor(hidden[:, s % 3, :], hidden[:, s % 3, :], ps_cb[:], ALU.mult).then_inc(h_ready, 1)

        def evacuate(dve, g):
            dve.wait_ge(down_done, NJ * (g + 1) + CREDIT)
            if g:
                dve.wait_ge(x2_stored, BG * g)
            for m in range(KH):
                v = xT[:, m, bass.ts(g, GTOK)]
                last = nc.vector.scalar_tensor_tensor(v, ps_acc[:, m, :], tg[:, 1:2], v, ALU.mult, ALU.add)
            last.then_inc(evac_ready, 1)

        @block.vector
        def _(dve):
            dve.sem_inc(prod_ready, CREDIT)
            dve.sem_inc(h_ready, CREDIT)
            works = (*pairs, one)
            for w in works:
                nc.vector.memset(w.k[:, :, 0:1], NEG)
                nc.vector.memset(w.kv[:, :, 0:1], 0.0)
                nc.vector.memset(w.e34[:, :, 0:1], 0.0)
                last = nc.vector.memset(w.dec, 0.0)
            last.then_inc(setup_step, 1)
            heads = [head_chain(dve, pairs[i], i) for i in range(2)]
            tails = [tail_chain(dve, pairs[i], i) for i in range(2)]
            for i in range(2):
                dve.wait_ge(x0_loaded[i], 16)
                head_dve_stats(dve, heads[i], pairs[i], PAIR * i, i)
            dve.wait_ge(gates_ready, 1)
            dve.wait_ge(setup_step, 1)
            nc.vector.tensor_scalar(decay[:], decay[:], -1.0, None, ALU.mult).then_inc(setup_step, 1)
            dve.wait_ge(setup_step, 2)
            for w in works:
                for kh in range(KH):
                    seg = w.dec[:, kh * w.nb:(kh + 1) * w.nb, :]
                    last = nc.vector.tensor_scalar(seg, seg, decay[:, kh:kh + 1], None, ALU.add)
            last.then_inc(setup_step, 1)
            dve.wait_ge(setup_step, 3)
            for w in works:
                last = nc.vector.memset(w.dec[:, :, 0:1], 2 * NEG)
            last.then_inc(setup_step, 1)
            for i in range(2):
                head_dve_norm(dve, heads[i], pairs[i], PAIR * i, i)
            nc.vector.tensor_scalar(tg[:, 1:2], tg[:, 1:2], 1.0 / WSCALE, None, ALU.mult)
            nc.vector.tensor_scalar(tg[:, 2:3], par[:, 6:7], 0.0, None, ALU.is_ge)
            nc.vector.tensor_scalar(tg[:, 3:4], par[:, 6:7], 0.0, None, ALU.is_lt)
            nc.vector.scalar_tensor_tensor(gate_lo[:], gate_w[:], WSCALE, gate_hi[:], ALU.mult,
                                           ALU.subtract).then_inc(gate_split, 1)
            dve.wait_ge(setup_step, 4)
            dve.wait_ge(gate_split, 1)

            for i in range(2):
                head_dve_max(dve, heads[i], pairs[i], i)
                head_dve_ends(dve, heads[i], pairs[i], i)
            for i in range(2):
                head_dve_sums(dve, heads[i], pairs[i], i)
            ch = head_chain(dve, one, 2)
            dve.wait_ge(xrest_loaded, 7 * 16)
            head_dve_stats(dve, ch, one, BG, 2)
            for i in range(2):
                head_dve_out(dve, heads[i], pairs[i], PAIR * i, i)
            head_dve_norm(dve, ch, one, BG, 2)
            for i in range(2):
                tail_dve_stats(dve, tails[i], pairs[i], i)
            for i in range(2):
                tail_dve_norm(dve, tails[i], pairs[i], i)
            head_dve_max(dve, ch, one, 2)
            for i in range(2):
                tail_dve_logits(dve, tails[i], pairs[i], i)
            head_dve_ends(dve, ch, one, 2)
            for i in range(2):
                tail_dve_route(dve, tails[i], pairs[i], i)
            unit_dve_prod(dve, 0, 0)
            head_dve_sums(dve, ch, one, 2)
            unit_dve_h(dve, 0, 0)
            unit_dve_prod(dve, 1, 1)
            head_dve_out(dve, ch, one, BG, 2)

            def step(t, opens, prep, tail, head, ending):
                b, ci = t + BG, t + 2
                ct, ch = tail_chain(dve, one, ci), head_chain(dve, one, ci + 1)
                for s in range(UPS):
                    n = UPS * t + s
                    if not ending or s < UPS - 1:
                        unit_dve_h(dve, n + 1, s + 1)
                    if opens and s == 0 and t > 0:
                        evacuate(dve, t // SPG - 1)
                    if tail and s == 0:
                        tail_dve_stats(dve, ct, one, ci)
                    if head and s == 0:
                        head_dve_stats(dve, ch, one, b + 1, ci + 1)
                    if tail and s == 0:
                        tail_dve_norm(dve, ct, one, ci)
                    if head and s == 0:
                        head_dve_norm(dve, ch, one, b + 1, ci + 1)
                    if head and s == 1:
                        head_dve_max(dve, ch, one, ci + 1)
                    if tail and s == 2:
                        tail_dve_logits(dve, ct, one, ci)
                    if head and s == 2:
                        head_dve_ends(dve, ch, one, ci + 1)
                    if tail and s == 3:
                        tail_dve_route(dve, ct, one, ci)
                    if head and s == 4:
                        head_dve_sums(dve, ch, one, ci + 1)
                    if head and s == 5:
                        head_dve_out(dve, ch, one, b + 1, ci + 1)
                    if not ending or s < UPS - 2:
                        unit_dve_prod(dve, n + 2, s + 2)

            run_steps(dve, step)
            evacuate(dve, NG - 1)

        def head_pe_keys(pe, w, ci):
            pe.wait_ge(xn1_ready, ci + 1)
            for i in range(w.nb):
                for kh in range(KH):
                    last = nc.tensor.transpose(w.ps_kT[:, kh * w.nb + i, :], w.xn[:, i, kh * P:(kh + 1) * P], ident[:])
            last.then_inc(kT_ready, 1)

        def head_pe_natural(pe, w, b, ci):
            pe.wait_ge(x2_ready, ci + 1)
            if w.nb == 1:
                pe.wait_ge(comb_ready, ci)
            for i in range(w.nb):
                for kh in range(KH):
                    src = xT[:, kh, (b + i) * T:(b + i + 1) * T] if w.x2 is None else w.x2[:, kh, :]
                    last = nc.tensor.transpose(w.ps_nat[:, i, kh * P:(kh + 1) * P], src, ident[:])
            last.then_inc(nat_ready, 1)

        def tail_pe_normalised(pe, w, ci):
            pe.wait_ge(xn2_ready, ci + 1)
            for i in range(w.nb):
                for kh in range(KH):
                    last = nc.tensor.transpose(w.ps_xnT[:, kh * w.nb + i, :], w.xn2[:, i, kh * P:(kh + 1) * P], ident[:])
            last.then_inc(xnT_ready, 1)

        def tail_pe_logits(pe, w, b, ci, keys):
            pe.wait_ge(xl_ready, ci + 1)
            if keys is not None:
                pe.wait_ge(k_ready, keys)
            for i in range(w.nb):
                tok = bass.ds((b + i) * T, T)
                for kh in range(KH):
                    for p, (xx, gw) in enumerate(((xn_hi, gate_hi), (xn_lo, gate_hi), (xn_hi, gate_lo))):
                        last = nc.tensor.matmul(w.ps_lg[:, i, :], xx[:, kh, tok], gw[:, kh, :],
                                                start=(kh == 0 and p == 0), stop=(kh == KH - 1 and p == 2))
            last.then_inc(lg_ready, 1)

        def tail_pe_comb(pe, w, ci):
            pe.wait_ge(c2_ready, ci + 1)
            lone_wait(pe)
            for i in range(w.nb):
                last = nc.tensor.transpose(w.ps_cT[:, i, :], w.c2[:, i, :, :].rearrange("p a e -> p (a e)"), ident16[:])
            last.then_inc(cT_ready, 1)

        def gate_up(pe, n, s, j, g):
            pe.wait_ge(prod_ready, n - 1 + CREDIT)
            for gu in range(2):
                for kh in range(KH):
                    col = bass.ds(j * WT_COLS + (kh * 2 + gu) * P, P)
                    tok = bass.ds(g * GTOK, GTOK)
                    for i, (w, xx) in enumerate(((w_hi, xn_hi), (w_hi, xn_lo), (w_lo, xn_hi))):
                        last = nc.tensor.matmul(ps_gu[:, s % 2, gu, :], w[:, col], xx[:, kh, tok],
                                                start=(kh == 0 and i == 0), stop=(kh == KH - 1 and i == 2))
            last.then_inc(gu_done, 1)

        def spread(pe, n, j, g):
            pe.wait_ge(h_ready, n + CREDIT)
            nc.tensor.matmul(ps_cb[:], expert_of[:].rearrange("p e i -> p (e i)")[:, bass.ds(j * P, P)],
                             combT[:, bass.ds(g * GTOK, GTOK)], start=True, stop=True).then_inc(cb_done, 1)

        def down(pe, n, s, j, last_of_group):
            pe.wait_ge(hl_ready, n + 1 + CREDIT)
            for m in range(KH):
                col = bass.ds(j * WT_COLS + 2 * KH * P + m * P, P)
                for i, (w, h) in enumerate(((w_hi, h_hi), (w_hi, h_lo), (w_lo, h_hi))):
                    last = nc.tensor.matmul(ps_acc[:, m, :], w[:, col], h[:, s % 3, :], start=False,
                                            stop=last_of_group and i == 2, skip_group_check=True)
            last.then_inc(down_done, 1)

        def open_group(pe, g):
            if g:
                pe.wait_ge(evac_ready, g)
            for m in range(KH):
                nc.tensor.matmul(ps_acc[:, m, :], zeros16[:], xn_hi[:, 0, 0:GTOK], start=True, stop=False,
                                 skip_group_check=True)

        @block.tensor
        def _(pe):
            pe.sem_inc(down_done, CREDIT)
            pe.wait_ge(consts_ready, 1)
            for i in range(2):
                head_pe_keys(pe, pairs[i], i)
            for i in range(2):
                head_pe_natural(pe, pairs[i], PAIR * i, i)
            head_pe_keys(pe, one, 2)
            for i in range(2):
                tail_pe_normalised(pe, pairs[i], i)
            pe.wait_ge(gate_split, 1)
            for i in range(2):
                tail_pe_logits(pe, pairs[i], PAIR * i, i, 3 * i or None)
            pe.wait_ge(w_ready, 1)
            gate_up(pe, 0, 0, 0, 0)
            for i in range(2):
                tail_pe_comb(pe, pairs[i], i)
            pe.wait_ge(w_ready, 2)
            gate_up(pe, 1, 1, 1, 0)
            pe.wait_ge(consts_ready, 2)
            pe.wait_ge(comb_ready, 2)
            spread(pe, 0, 0, 0)
            spread(pe, 1, 1, 0)

            def step(t, opens, prep, tail, head, ending):
                b, ci = t + BG, t + 2
                for s in range(UPS):
                    n = UPS * t + s
                    begins = not ending or s < UPS - 2
                    t2, s2 = (t, s + 2) if s < UPS - 2 else (t + 1, s + 2 - UPS)
                    j2, g2 = UPS * (t2 % SPG) + s2, t2 // SPG
                    if begins:
                        if tail and s == UPS - 2:
                            pe.wait_ge(xl_ready, BG * g2 + 2)
                        if prep or (isinstance(t, int) and t == SPG - 1 and s < UPS - 2):
                            pe.wait_ge(w_ready, n + 3)
                        gate_up(pe, n + 2, s, j2, g2)
                    if tail and s == 0 and isinstance(t, int) and t == 0:
                        head_pe_natural(pe, one, b, ci)
                    if tail and s == 4:
                        tail_pe_comb(pe, one, ci)
                    if opens and s == 0:
                        open_group(pe, t // SPG)
                    down(pe, n, s, UPS * (t % SPG) + s, s == UPS - 1)
                    if tail and s == 0:
                        tail_pe_normalised(pe, one, ci)
                    if head and s == 0:
                        head_pe_keys(pe, one, ci + 1)
                    if tail and s == 1:
                        tail_pe_logits(pe, one, b, ci, ci + 2 if head else None)
                    if head and s == 5:
                        head_pe_natural(pe, one, b + 1, ci + 1)
                    if begins:
                        if tail and s == UPS - 2:
                            pe.wait_ge(comb_ready, BG * g2 + 2)
                        spread(pe, n + 2, j2, g2)

            run_steps(pe, step)


def kernel(x, ctx_2048, g_xattn, g_ffn, L0_xattn_time_decay, L0_xattn_time_first, L0_ffn_gate_weight,
           L0_ffn_gate_up_proj, L0_ffn_down_proj, L0_ffn_layer_alpha):
    import numpy as np
    import concourse.bacc as bacc
    from concourse.bass_utils import run_bass_kernel_spmd

    def transposed(a):
        a = np.asarray(a).reshape(NG, GTOK, KH, P)
        return np.ascontiguousarray(a.transpose(0, 3, 2, 1))

    def per_channel(v):
        return np.asarray(v).reshape(KH, P).T

    def everywhere(v):
        return np.broadcast_to(np.asarray(v).reshape(1, 1), (P, 1))

    params = np.ascontiguousarray(np.concatenate(
        [per_channel(L0_xattn_time_decay), per_channel(L0_xattn_time_first), everywhere(g_xattn), everywhere(g_ffn),
         everywhere(L0_ffn_layer_alpha), everywhere(L0_ffn_layer_alpha)], axis=1))
    gate_up = np.asarray(L0_ffn_gate_up_proj).reshape(NE, 2, INTER, KH, P)
    gate_up = gate_up.transpose(1, 0, 2, 3, 4).reshape(2, NJ, P, KH, P)
    gate_up = gate_up.transpose(1, 4, 3, 0, 2).reshape(NJ, P, 2 * KH * P)
    down = np.asarray(L0_ffn_down_proj).transpose(0, 2, 1).reshape(NJ, P, C)
    weights = np.ascontiguousarray(np.concatenate([gate_up, down], axis=2))
    gate_wt = np.ascontiguousarray(np.asarray(L0_ffn_gate_weight).reshape(NE, KH, P).transpose(2, 1, 0))

    arrays = {"in_x": np.ascontiguousarray(x), "in_xt": transposed(x), "in_ctx": transposed(ctx_2048),
              "in_params": params, "in_gate": gate_wt, "in_weights": weights}
    nc = bacc.Bacc("TRN2", target_bir_lowering=False, num_devices=1)
    args = [nc.dram_tensor(name, a.shape, mybir.dt.from_np(a.dtype), kind="ExternalInput").ap()
            for name, a in arrays.items()]
    args.append(nc.dram_tensor("out_y", (NG, P, KH, GTOK), F32, kind="ExternalOutput").ap())
    rwkv_moe_kernel(nc, *args)
    r = run_bass_kernel_spmd(nc, [arrays], core_ids=[0])
    y = r.results[0]["out_y"]
    return y.transpose(0, 3, 2, 1).reshape(B, T, C)
```

```python
from contextlib import ExitStack

import concourse.bass as bass
from concourse import mybir

F32 = mybir.dt.float32
F16 = mybir.dt.float16
ALU = mybir.AluOpType
ACT = mybir.ActivationFunctionType
AX = mybir.AxisListType.X

P = 128
B, T, C = 16, 128, 256
KH = C // P
NTOK = B * T
BG = 4
GTOK = BG * T
NG = B // BG
NE, INTER = 32, 96
TAU = 0.05
NJ = NE * INTER // P
WT_COLS = 2 * KH * P + C
UPS = 6
SPG = NJ // UPS
NSTEP = NG * SPG
EPS = 1e-5
NEG = -1e38

WSCALE = 64.0
XSCALE = 256.0
GU_UNSCALE = 1.0 / (WSCALE * XSCALE)

CREDIT = 3
PAIR = 2
LEAD = 9
TPS = (NJ - LEAD) // (SPG - 1)
RING = TPS
HEAD_LINKS, NORM_LINKS, ROUTE_LINKS = 5, 2, 15


class Chain:

    def __init__(self, eng, sem, base):
        self.eng, self.sem, self.base, self.n = eng, sem, base, 0

    def link(self, ins):
        self.n += 1
        ins.then_inc(self.sem, 1)
        self.eng.wait_ge(self.sem, self.base + self.n)


def flat(a):
    return a.rearrange("p s t -> p (s t)")


def rwkv_moe_kernel(nc, x, xt, ctx, params, gate_wt, weights, out, comb_dram):
    with ExitStack() as st:
        def sb(name, shape, dt):
            return st.enter_context(nc.sbuf_tensor(name, shape, dt))

        def sem(name):
            return st.enter_context(nc.semaphore(name))

        w_hi = sb("w_hi", [P, NJ * WT_COLS], F16)
        w_lo = sb("w_lo", [P, NJ * WT_COLS], F16)
        w_stage = sb("w_stage", [P, RING, WT_COLS], F32)
        x_nat = sb("x_nat", [P, B, C], F32)
        xT = sb("xT", [P, KH, NTOK], F32)
        ctxT = sb("ctxT", [P, KH, NTOK], F32)
        xn_hi = sb("xn_hi", [P, KH, NTOK], F16)
        xn_lo = sb("xn_lo", [P, KH, NTOK], F16)
        comb_of = sb("comb_of", [P, 3, GTOK], F32)
        hidden = sb("hidden", [P, 3, GTOK], F32)
        h_hi = sb("h_hi", [P, 3, GTOK], F16)
        h_lo = sb("h_lo", [P, 3, GTOK], F16)
        par = sb("par", [P, 8], F32)
        gate_w = sb("gate_w", [P, KH, NE], F32)
        gate_hi = sb("gate_hi", [P, KH, NE], F16)
        gate_lo = sb("gate_lo", [P, KH, NE], F16)
        ident = sb("ident", [P, P], F32)
        ones32 = sb("ones32", [P, NE], F32)
        decay = sb("decay", [P, KH], F32)
        tg = sb("tg", [P, 4], F32)
        table_warm = sb("table_warm", [P, 1], F32)
        halfpow = sb("halfpow", [P, BG], F32)

        class Work:

            def __init__(self, nb, first_call, b0, take, tag):
                def small(name, cols):
                    return sb(name + tag, [P, nb, cols], F32)[:]

                self.nb, self.S = nb, KH * nb
                self.first_call = first_call
                S = self.S
                self.k, self.pp, self.dec = take([P, S, T + 1]), take([P, S, T + 1]), take([P, S, T + 1])
                self.kv, self.aa, self.bb = take([P, S, T + 1]), take([P, S, T + 1]), take([P, S, T + 1])
                self.e12 = take([P, 2 * S, T])
                self.e34 = sb(f"e34{tag}", [P, 2 * S, T + 1], F32)[:]
                self.t2 = sb(f"t2{tag}", [P, S, T], F32)[:]
                self.xn = x_nat[:, b0:b0 + nb, :] if nb > 1 else sb(f"xn{tag}", [P, 1, C], F32)[:]
                self.xn2 = flat(self.t2).rearrange("p (b c) -> p b c", c=C)
                self.x2 = None if nb > 1 else sb(f"x2{tag}", [P, S, T], F32)[:]
                self.xf = self.e12 if nb > 1 else sb(f"xf{tag}", [P, S, T], F32)[:]
                self.st, self.mv, self.ve, self.rs = small("st", 6), small("mv", 2), small("ve", 1), small("rs", 1)
                self.st2, self.mv2, self.ve2, self.rs2 = small("st2", 6), small("mv2", 2), small("ve2", 1), small("rs2", 1)
                self.head_step = sem(f"head_step{tag}")
                self.norm1_step, self.norm2_step = sem(f"norm1_step{tag}"), sem(f"norm2_step{tag}")
                self.pool_step = sem(f"pool_step{tag}")

        class Router:

            def __init__(self, nb, first_call, ps, tag):
                def small(name, cols):
                    return sb(name + tag, [P, nb, cols], F32)[:]

                self.nb, self.first_call = nb, first_call
                self.lg, self.top = small("lg", NE), small("top", 1)
                self.E, self.e8, self.left = small("E", NE), small("e8", 8), small("left", NE)
                self.s8, self.r8, self.vn = small("s8", 1), small("r8", 1), small("vn", NE)
                self.act, self.any = small("act", NE), small("any", 1)
                self.tgt, self.eq, self.cs = small("tgt", 1), small("eq", NE), small("cs", NE)
                self.wg, self.ws, self.rw = small("wg", NE), small("ws", 1), small("rw", 1)
                self.c = small("c", NE)
                self.comb = sb(f"comb{tag}", [NE, nb * T], F32)[:]
                self.ps_lg = ps[:, 0:nb * NE].rearrange("p (b e) -> p b e", e=NE)
                self.ps_cT = ps[0:NE, 0:nb * T].rearrange("p (b t) -> p b t", t=T)
                self.route_step = sem(f"route_step{tag}")

        late = {0: [w_hi, NJ // 2 * WT_COLS], 1: [w_lo, NJ // 2 * WT_COLS]}

        def take_late(shape):
            n = shape[1] * shape[2]
            for key in (0, 1):
                buf, at = late[key]
                if at + 2 * n <= NJ * WT_COLS:
                    late[key][1] = at + 2 * n
                    return buf[:, at:at + 2 * n].bitcast(F32).rearrange("p (s t) -> p s t", s=shape[1])
            raise ValueError("the startup's buffers don't fit")

        counter = [0]

        def take_own(shape):
            counter[0] += 1
            return sb(f"work{counter[0]}", shape, F32)[:]

        pairs = [Work(PAIR, i, PAIR * i, take_late, f"_p{i}") for i in range(2)]
        one = Work(1, 2, None, take_own, "_1")

        ps_gu = st.enter_context(nc.psum_tensor("ps_gu", [P, 2, 2, GTOK], F32))
        ps_acc = st.enter_context(nc.psum_tensor("ps_acc", [P, KH, GTOK], F32))
        ps_route = st.enter_context(nc.psum_tensor("ps_route", [P, GTOK], F32))
        ps_misc = st.enter_context(nc.psum_tensor("ps_misc", [P, GTOK], F32))

        def psum_views(w, keys, nat, xnT):
            w.ps_kT = keys.rearrange("p (s t) -> p s t", t=T)
            w.ps_nat = nat.rearrange("p (b c) -> p b c", c=C)
            w.ps_xnT = xnT.rearrange("p (s t) -> p s t", t=T)

        for i in range(2):
            psum_views(pairs[i], ps_gu[:, i, 0, :], ps_gu[:, i, 1, :], ps_gu[:, i, 0, :])
        psum_views(one, ps_misc[:, C:2 * C], ps_misc[:, 0:C], ps_misc[:, 0:C])
        group = Router(BG, 0, ps_route, "_g")
        single = Router(1, 1, ps_route, "_s")

        par_loaded = sem("par_loaded")
        x0_loaded = [sem(f"x0_loaded{i}") for i in range(2)]
        xt0_loaded = sem("xt0_loaded")
        xrest_loaded = sem("xrest_loaded")
        w_loaded = [sem(f"w_loaded{i}") for i in range(RING)]
        passed = sem("passed")
        consts_ready = sem("consts_ready")
        const_step = sem("const_step")
        pads_set = sem("pads_set")
        decay_step = sem("decay_step")
        dec_ready = sem("dec_ready")
        gates_ready = sem("gates_ready")
        gate_split = sem("gate_split")
        wh_ready = sem("wh_ready")
        w_ready = sem("w_ready")
        var1_ready = sem("var1_ready")
        rs1_ready = sem("rs1_ready")
        xn1_ready = sem("xn1_ready")
        kT_ready = sem("kT_ready")
        k_ready = sem("k_ready")
        d34_ready, d12_ready = sem("d34_ready"), sem("d12_ready")
        d4_ready = sem("d4_ready")
        relu_done = sem("relu_done")
        e34_ready, e12_ready = sem("e34_ready"), sem("e12_ready")
        kv_ready, t2_ready = sem("kv_ready"), sem("t2_ready")
        sums_ready = sem("sums_ready")
        num_ready = sem("num_ready")
        x2_ready = sem("x2_ready")
        x2_stored = sem("x2_stored")
        nat_ready = sem("nat_ready")
        var2_ready, rs2_ready, xn2_ready = sem("var2_ready"), sem("rs2_ready"), sem("xn2_ready")
        xnT_ready = sem("xnT_ready")
        xh_ready = sem("xh_ready")
        xf_copied = sem("xf_copied")
        xl_ready = sem("xl_ready")
        lg_ready = sem("lg_ready")
        below_ready = sem("below_ready")
        exp_ready = sem("exp_ready")
        c_ready = sem("c_ready")
        cT_ready, comb_ready = sem("cT_ready"), sem("comb_ready")
        comb_written = sem("comb_written")
        gu_done = sem("gu_done")
        comb_loaded = [sem(f"comb_loaded{i}") for i in range(3)]
        silu_ready = sem("silu_ready")
        prod_ready = sem("prod_ready")
        h_ready = sem("h_ready")
        hh_ready = sem("hh_ready")
        hl_ready = sem("hl_ready")
        down_done = sem("down_done")
        evac_ready = sem("evac_ready")
        out_done = sem("out_done")

        block = st.enter_context(nc.Block())

        def lone_wait(eng):
            eng.sem_inc(passed, 1)

        def run_steps(eng, step, straight=False):
            step(0, True, 2, 2)
            if straight:
                step(1, True, 2, 2)
                step(2, True, 2, 2)
            else:
                with eng.Fori(1, SPG - 1) as t:
                    step(t, True, 2, 2)
            step(SPG - 1, False, 2, 2)
            step(SPG, False, 2, 2)
            with eng.Fori(SPG + 1, 2 * SPG - 1) as t:
                step(t, False, 2, 2)
            step(2 * SPG - 1, False, 2, 2)
            step(2 * SPG, False, 2, 2)
            step(2 * SPG + 1, False, 2, 2)
            step(2 * SPG + 2, False, 2, 1)
            step(3 * SPG - 1, False, 1, 0)
            step(3 * SPG, False, 0, 0)
            with eng.Fori(3 * SPG + 1, NSTEP - 1) as t:
                step(t, False, 0, 0)
            step(NSTEP - 1, False, 0, 0)


        def is_(t, k):
            return isinstance(t, int) and t == k

        def opens(t):
            return isinstance(t, int) and t % SPG == 0

        def closes(t):
            return isinstance(t, int) and t % SPG == SPG - 1

        def split_here(s, prep):
            return {0: [0], 2: [1], 3: [2, 3], 5: [4]}.get(s, []) if prep else []

        def unit(t, s, ahead):
            t2, s2 = (t, s + ahead) if s + ahead < UPS else (t + 1, s + ahead - UPS)
            if isinstance(t2, int) and t2 == NSTEP:
                return None
            return t2, s2

        def load_weights(sp, j):
            if j >= RING:
                sp.wait_ge(w_ready, j - RING + 1)
            sp.dma_start(w_stage[:, j % RING, :], weights[j]).then_inc(w_loaded[j % RING], 16)

        def write_comb(sp, r, b, rc):
            sp.wait_ge(comb_ready, rc + 1)
            lone_wait(sp)
            sp.dma_start(comb_dram[:, bass.ds(b * T, r.nb * T)], r.comb).then_inc(comb_written, 16)

        def load_comb(sp, t, s):
            first = INTER - P * s % INTER
            expert = UPS * P // INTER * (t % SPG) + P * s // INTER
            for e, lo, hi in ((expert, 0, first), (expert + 1, first, P)):
                row = comb_dram[bass.ds(e, 1), bass.ds((t // SPG) * GTOK, GTOK)]
                sp.dma_start(comb_of[lo:hi, s % 3, :], row.broadcast_to([hi - lo, GTOK])).then_inc(comb_loaded[s % 3], 16)

        def store_group(sp, g):
            for m in range(KH):
                sp.wait_ge(evac_ready, KH * g + m + 1)
                sp.dma_start(out[g, :, m, :], xT[:, m, bass.ts(g, GTOK)]).then_inc(out_done, 16)

        @block.sync
        def _(sp):
            for i in range(2):
                sp.dma_start(x_nat[:, PAIR * i:PAIR * i + PAIR, :],
                             x[PAIR * i:PAIR * i + PAIR].rearrange("b t c -> t b c")).then_inc(x0_loaded[i], 16)
            sp.dma_start(ctxT[:, :, 0:GTOK], ctx[0]).then_inc(xt0_loaded, 16)
            sp.dma_start(xT[:, :, 0:GTOK], xt[0]).then_inc(xt0_loaded, 16)
            for j in range(LEAD + 2):
                load_weights(sp, j)
                if j == 2:
                    sp.dma_start(x_nat[:, BG:B, :], x[BG:B].rearrange("b t c -> t b c")).then_inc(xrest_loaded, 16)
                    for g in range(1, NG):
                        sp.dma_start(xT[:, :, bass.ts(g, GTOK)], xt[g]).then_inc(xrest_loaded, 16)
                        sp.dma_start(ctxT[:, :, bass.ts(g, GTOK)], ctx[g]).then_inc(xrest_loaded, 16)
            write_comb(sp, group, 0, 0)
            sp.wait_ge(comb_written, 16)
            for n in range(3):
                load_comb(sp, 0, n)
            for j in range(LEAD + 2, LEAD + TPS - 1):
                load_weights(sp, j)

            def step(t, prep, now, then):
                for s in range(UPS):
                    n = UPS * t + s
                    if now and s == (4 if is_(t, 0) else 3):
                        write_comb(sp, single, t + BG, t + 1)
                        sp.wait_ge(comb_written, 16 * (t + 2))
                        lone_wait(sp)
                    if unit(t, s, 3):
                        sp.wait_ge(h_ready, n + 1 + CREDIT)
                        lone_wait(sp)
                        load_comb(sp, *unit(t, s, 3))
                    if prep:
                        for i in {0: [-1], 1: [0], 3: [1], 4: [2], 5: [3]}.get(s, []):
                            if LEAD + TPS * (t + 1) + i < NJ:
                                load_weights(sp, LEAD + TPS * (t + 1) + i)
                    if opens(t) and t > 0 and s == 1:
                        store_group(sp, t // SPG - 1)

            run_steps(sp, step, straight=True)
            store_group(sp, NG - 1)
            sp.wait_ge(out_done, 16 * KH * NG)

        def weight_high(act, j, slot, arrivals):
            act.wait_ge(w_loaded[slot], 16 * arrivals)
            stage = w_stage[:, slot, :]
            nc.scalar.activation(w_hi[:, bass.ds(j * WT_COLS, WT_COLS)], stage, ACT.Copy, scale=WSCALE)
            nc.scalar.activation(stage, stage, ACT.Copy, scale=WSCALE).then_inc(wh_ready, 1)

        def head_act_k(act, w, ci):
            act.wait_ge(kT_ready, ci + 1)
            if w.nb == 1:
                act.wait_ge(d12_ready, ci)
            nc.scalar.copy(w.k[:, :, 1:], w.ps_kT).then_inc(k_ready, 1)

        def head_act_e34(act, w, ci):
            act.wait_ge(d34_ready, ci + 1)
            if w.nb > 1:
                act.wait_ge(d4_ready, ci + 1)
            nc.scalar.activation(w.e34[:, :, 1:], w.e34[:, :, 1:], ACT.Exp).then_inc(e34_ready, 1)

        def head_act_relu(act, w, ci):
            act.wait_ge(d12_ready, ci + 1)
            d = w.e12[:, w.S:, :]
            nc.scalar.activation(w.e12[:, 0:w.S, :], d, ACT.Relu)
            nc.scalar.activation(d, d, ACT.Relu, scale=-1.0).then_inc(relu_done, 1)

        def head_act_e12(act, w, ci):
            act.wait_ge(relu_done, ci + 1)
            nc.scalar.activation(w.e12, w.e12, ACT.Exp, scale=-1.0).then_inc(e12_ready, 1)

        def head_act_store(act, w, b, ci):
            act.wait_ge(x2_ready, ci + 1)
            nc.scalar.copy(xT[:, :, bass.ds(b * T, T)], w.x2).then_inc(x2_stored, 1)

        def tail_act_x(act, w, b, ci):
            act.wait_ge(xnT_ready, ci + 1)
            if w.nb == 1:
                act.wait_ge(xl_ready, ci)
            nc.scalar.activation(w.xf[:, 0:w.S, :], w.ps_xnT, ACT.Copy, scale=XSCALE).then_inc(xf_copied, 1)
            act.wait_ge(xf_copied, ci + 1)
            nc.scalar.copy(xn_hi[:, :, bass.ds(b * T, w.nb * T)],
                           w.xf[:, 0:w.S, :].rearrange("p (k s) t -> p k (s t)", k=KH)).then_inc(xh_ready, 1)

        def route_act_exp(act, r, rc):
            act.wait_ge(below_ready, rc + 1)
            nc.scalar.activation(r.E, r.lg, ACT.Exp, scale=GU_UNSCALE).then_inc(exp_ready, 1)

        def route_act_comb(act, r, rc):
            act.wait_ge(cT_ready, rc + 1)
            if r.nb == 1:
                act.wait_ge(comb_written, 16 * rc)
            nc.scalar.activation(r.comb, flat(r.ps_cT), ACT.Copy, scale=GU_UNSCALE).then_inc(comb_ready, 1)

        def unit_act_silu(act, n, s):
            act.wait_ge(gu_done, n + 1)
            act.wait_ge(hl_ready, n - 2 + CREDIT)
            nc.scalar.activation(hidden[:, s % 3, :], ps_gu[:, s % 2, 0, :], ACT.Silu,
                                 scale=GU_UNSCALE).then_inc(silu_ready, 1)

        def unit_act_high(act, n, s):
            act.wait_ge(h_ready, n + 1 + CREDIT)
            act.wait_ge(down_done, n - 2 + CREDIT)
            nc.scalar.copy(h_hi[:, s % 3, :], hidden[:, s % 3, :]).then_inc(hh_ready, 1)

        def spread_decay(w):
            for kh in range(KH):
                seg = w.dec[:, kh * w.nb:(kh + 1) * w.nb, 1:]
                last = nc.scalar.activation(seg, seg, ACT.Identity, bias=decay[:, kh:kh + 1])
            last.then_inc(dec_ready, 1)

        @block.scalar
        def _(act):
            act.dma_start(par[:], params).then_inc(par_loaded, 16)
            act.dma_start(gate_w[:], gate_wt).then_inc(par_loaded, 16)
            act.wait_ge(pads_set, 1)
            nc.scalar.activation(table_warm[:], one.dec[:, 0, 1:2], ACT.Exp)
            act.wait_ge(par_loaded, 2 * 16)
            nc.scalar.activation(decay[:], par[:, 0:2], ACT.Exp).then_inc(decay_step, 1)
            act.wait_ge(decay_step, 1)
            nc.scalar.activation(decay[:], decay[:], ACT.Copy, scale=-1.0).then_inc(decay_step, 1)
            act.wait_ge(decay_step, 2)
            for i in range(2):
                spread_decay(pairs[i])
            for i in range(2):
                head_act_k(act, pairs[i], i)
            spread_decay(one)
            nc.scalar.activation(tg[:, 0:2], par[:, 4:6], ACT.Tanh)
            nc.scalar.activation(gate_hi[:], gate_w[:], ACT.Copy, scale=WSCALE).then_inc(gates_ready, 1)
            for i in range(2):
                head_act_e34(act, pairs[i], i)
                head_act_relu(act, pairs[i], i)
                head_act_e12(act, pairs[i], i)
            for j in range(6):
                weight_high(act, j, j % RING, j // RING + 1)
            for i in range(2):
                tail_act_x(act, pairs[i], PAIR * i, i)
            head_act_k(act, one, 2)
            head_act_e34(act, one, 2)
            route_act_exp(act, group, 0)
            head_act_relu(act, one, 2)
            head_act_e12(act, one, 2)
            weight_high(act, 6, 6 % RING, 6 // RING + 1)
            unit_act_silu(act, 0, 0)
            weight_high(act, 7, 7 % RING, 7 // RING + 1)
            route_act_comb(act, group, 0)
            unit_act_silu(act, 1, 1)
            weight_high(act, 8, 8 % RING, 8 // RING + 1)
            unit_act_silu(act, 2, 2)
            head_act_store(act, one, BG, 2)
            unit_act_high(act, 0, 0)
            unit_act_high(act, 1, 1)

            def step(t, prep, now, then):
                for s in range(UPS):
                    n = UPS * t + s
                    begun = unit(t, s, 2)
                    if begun and not (s == 0 and is_(t, 0)):
                        unit_act_silu(act, n + 2, s + 2)
                    if s == 1 and now:
                        route_act_exp(act, single, t + 1)
                    if s == 1 and now == 2:
                        head_act_e34(act, one, t + 3)
                        head_act_e12(act, one, t + 3)
                    if s == (4 if is_(t, 0) else 3) and now:
                        route_act_comb(act, single, t + 1)
                    if s == 0 and is_(t, 0):
                        head_act_k(act, one, 3)
                        tail_act_x(act, one, BG, 2)
                    for i in split_here(s, prep):
                        weight_high(act, TPS * t + LEAD + i, (LEAD + i) % RING, t + (LEAD + i) // RING + 1)
                    if s == 4 and then:
                        head_act_store(act, one, t + 5, t + 3)
                    if s == 5 and then == 2:
                        head_act_k(act, one, t + 4)
                    if s == 5 and then:
                        tail_act_x(act, one, t + 5, t + 3)
                    if begun:
                        unit_act_high(act, n + 2, s + 2)
                    if s == 0 and now == 2:
                        head_act_relu(act, one, t + 3)

            run_steps(act, step)

        def weight_low(pool, j, slot):
            pool.wait_ge(wh_ready, j + 1)
            lone_wait(pool)
            col = bass.ds(j * WT_COLS, WT_COLS)
            nc.gpsimd.tensor_tensor(w_lo[:, col], w_stage[:, slot, :], w_hi[:, col], ALU.subtract).then_inc(w_ready, 1)

        def rsqrt_pool(pool, ve, rs, ready, done, ci):
            pool.wait_ge(ready, ci + 1)
            nc.gpsimd.tensor_tensor(rs, ve, halfpow[:, 0:ve.shape[1]].unsqueeze(2), ALU.pow).then_inc(done, 1)

        def head_pool_v(pool, w, b, ci):
            S = w.S

            def by_half(a):
                return a.rearrange("p (k s) t -> p k s t", k=KH) if w.nb > 1 else a

            v = ctxT[:, :, bass.ds(b * T, w.nb * T)]
            if w.nb > 1:
                v = v.rearrange("p k (s t) -> p k s t", t=T)
                pool.wait_ge(xt0_loaded, 2 * 16)
            pool.wait_ge(e34_ready, ci + 1)
            lone_wait(pool)
            nc.gpsimd.tensor_tensor(by_half(w.kv[:, :, 1:]), by_half(w.e34[:, S:, 1:]), v, ALU.mult).then_inc(kv_ready, 1)
            pool.wait_ge(e12_ready, ci + 1)
            lone_wait(pool)
            nc.gpsimd.tensor_tensor(by_half(w.t2), by_half(w.e12[:, S:, :]), v, ALU.mult).then_inc(t2_ready, 1)

        def head_pool_d4(pool, w):
            pool.wait_ge(w.head_step, 1)
            nc.gpsimd.tensor_tensor(w.e34[:, w.S:, 1:], w.k[:, :, 1:], w.pp[:, :, 1:], ALU.subtract).then_inc(d4_ready, 1)

        def head_pool_out(pool, w):
            pool.wait_ge(w.head_step, HEAD_LINKS)
            v = xT[:, :, 0:PAIR * T].rearrange("p k (s t) -> p k s t", t=T)
            y = w.aa[:, :, 0:T].rearrange("p (k s) t -> p k s t", k=KH)
            nc.gpsimd.tensor_tensor(v, y, v, ALU.add).then_inc(x2_ready, 1)

        def head_pool_num(pool, w, ci):
            ch = Chain(pool, w.pool_step, ci - w.first_call)
            num = w.aa[:, :, 0:T]
            pool.wait_ge(sums_ready, ci + 1)
            pool.wait_ge(t2_ready, ci + 1)
            ch.link(nc.gpsimd.tensor_tensor(num, num, w.e12[:, 0:w.S, :], ALU.mult))
            nc.gpsimd.tensor_tensor(num, num, w.t2, ALU.add).then_inc(num_ready, 1)

        def tail_pool_x(pool, w, b, ci):
            pool.wait_ge(xh_ready, ci + 1)
            lone_wait(pool)
            col = bass.ds(b * T, w.nb * T)
            nc.gpsimd.tensor_tensor(xn_lo[:, :, col], w.xf[:, 0:w.S, :].rearrange("p (k s) t -> p k (s t)", k=KH),
                                    xn_hi[:, :, col], ALU.subtract).then_inc(xl_ready, 1)

        def unit_pool_low(pool, n, s):
            pool.wait_ge(hh_ready, n + 1)
            nc.gpsimd.tensor_tensor(h_lo[:, s % 3, :], hidden[:, s % 3, :], h_hi[:, s % 3, :],
                                    ALU.subtract).then_inc(hl_ready, 1)

        @block.gpsimd
        def _(pool):
            pool.sem_inc(hl_ready, CREDIT)
            nc.gpsimd.memset(halfpow[:], -0.5)
            nc.gpsimd.memset(ident[:], 0.0)
            nc.gpsimd.memset(ones32[:], 1.0).then_inc(const_step, 1)
            pool.wait_ge(const_step, 1)
            nc.gpsimd.affine_select(out=ident[:], in_=ident[:], compare_op=ALU.not_equal, fill=1.0, base=0,
                                    pattern=[[-1, P]], channel_multiplier=1).then_inc(consts_ready, 1)
            for i in range(2):
                rsqrt_pool(pool, pairs[i].ve, pairs[i].rs, var1_ready, rs1_ready, i)
            for i in range(2):
                head_pool_d4(pool, pairs[i])
            for i in range(2):
                head_pool_v(pool, pairs[i], PAIR * i, i)
            for i in range(2):
                head_pool_num(pool, pairs[i], i)
            weight_low(pool, 0, 0)
            head_pool_out(pool, pairs[0])
            for j in range(1, 3):
                weight_low(pool, j, j % RING)
            rsqrt_pool(pool, pairs[0].ve2, pairs[0].rs2, var2_ready, rs2_ready, 0)
            rsqrt_pool(pool, pairs[1].ve2, pairs[1].rs2, var2_ready, rs2_ready, 1)
            weight_low(pool, 3, 3)
            rsqrt_pool(pool, one.ve, one.rs, var1_ready, rs1_ready, 2)
            tail_pool_x(pool, pairs[0], 0, 0)
            rsqrt_pool(pool, one.ve, one.rs, var1_ready, rs1_ready, 3)
            tail_pool_x(pool, pairs[1], PAIR, 1)
            head_pool_v(pool, one, BG, 2)
            for j in range(4, 7):
                weight_low(pool, j, j % RING)
            head_pool_num(pool, one, 2)
            for j in range(7, LEAD):
                weight_low(pool, j, j % RING)
            unit_pool_low(pool, 0, 0)
            rsqrt_pool(pool, one.ve2, one.rs2, var2_ready, rs2_ready, 2)
            unit_pool_low(pool, 1, 1)

            def step(t, prep, now, then):
                for s in range(UPS):
                    n = UPS * t + s
                    if s == 1 and then == 2:
                        rsqrt_pool(pool, one.ve, one.rs, var1_ready, rs1_ready, t + 4)
                    if s == 1 and now == 2:
                        head_pool_v(pool, one, t + 5, t + 3)
                    if s == 4 and then:
                        rsqrt_pool(pool, one.ve2, one.rs2, var2_ready, rs2_ready, t + 3)
                    if s == 5 and then:
                        tail_pool_x(pool, one, t + 5, t + 3)
                    if s == 0 and is_(t, 0):
                        tail_pool_x(pool, one, BG, 2)
                    for i in split_here(s, prep):
                        weight_low(pool, TPS * t + LEAD + i, (LEAD + i) % RING)
                    if s == 2 and now == 2:
                        head_pool_num(pool, one, t + 3)
                    if unit(t, s, 2):
                        unit_pool_low(pool, n + 2, s + 2)

            run_steps(pool, step)

        def stats(ch, src, w, st_, mv, ve, ready):
            for i in range(w.nb):
                last = nc.vector.bn_stats(st_[:, i, :], src(i))
            ch.link(last)
            lone_wait(ch.eng)
            for i in range(w.nb):
                last = nc.vector.bn_aggr(mv[:, i, :], st_[:, i, :])
            ch.link(last)
            nc.vector.tensor_scalar(ve, mv[:, :, 1:2], EPS, None, ALU.add).then_inc(ready, 1)

        def normalise(dve, src, dst, w, mv, rs, pooled, ci, done):
            dve.wait_ge(pooled, ci + 1)
            for i in range(w.nb):
                last = nc.vector.tensor_scalar(dst(i), src(i), mv[:, i, 0:1], rs[:, i, :], ALU.subtract, ALU.mult)
            last.then_inc(done, 1)

        def head_chain(dve, w, ci):
            return Chain(dve, w.head_step, HEAD_LINKS * (ci - w.first_call))

        def norm_chain(dve, w, ci, step):
            return Chain(dve, step, NORM_LINKS * (ci - w.first_call))

        def route_chain(dve, r, rc):
            return Chain(dve, r.route_step, ROUTE_LINKS * (rc - r.first_call))

        def tokens(b):
            return lambda i: x_nat[:, bass.ds(b + i, 1), :].rearrange("p a c -> p (a c)")

        def head_dve_stats(dve, w, b, ci):
            stats(norm_chain(dve, w, ci, w.norm1_step), tokens(b), w, w.st, w.mv, w.ve, var1_ready)

        def head_dve_norm(dve, w, b, ci):
            if w.nb == 1:
                dve.wait_ge(kT_ready, ci)
            normalise(dve, tokens(b), lambda i: w.xn[:, i, :], w, w.mv, w.rs, rs1_ready, ci, xn1_ready)

        def head_dve_max(dve, ch, w, ci):
            S, nb = w.S, w.nb
            dve.wait_ge(k_ready, ci + 1)
            ch.link(nc.vector.tensor_tensor_scan(flat(w.pp), flat(w.dec), flat(w.k), NEG, ALU.add, ALU.max))
            before, after = w.pp[:, :, 0:T], w.pp[:, :, 1:]
            for kh in range(KH):
                seg = slice(kh * nb, (kh + 1) * nb)
                last = nc.vector.scalar_tensor_tensor(w.e34[:, seg, 1:], before[:, seg, :], decay[:, kh:kh + 1],
                                                      after[:, seg, :], ALU.add, ALU.subtract)
            if nb > 1:
                last.then_inc(d34_ready, 1)
            else:
                nc.vector.tensor_tensor(w.e34[:, S:, 1:], w.k[:, :, 1:], after, ALU.subtract).then_inc(d34_ready, 1)

        def head_dve_ends(dve, w, ci):
            S, nb = w.S, w.nb
            if nb == 1:
                dve.wait_ge(num_ready, ci)
            for kh in range(KH):
                lo, hi = kh * nb, (kh + 1) * nb
                last = nc.vector.scalar_tensor_tensor(w.e12[:, S + lo:S + hi, :], w.k[:, lo:hi, 1:],
                                                      par[:, 2 + kh:3 + kh], w.pp[:, lo:hi, 0:T], ALU.add, ALU.subtract)
            last.then_inc(d12_ready, 1)

        def head_dve_sums(dve, ch, w, ci):
            e3, e4 = flat(w.e34[:, 0:w.S, :]), flat(w.e34[:, w.S:, :])
            dve.wait_ge(e34_ready, ci + 1)
            nc.vector.tensor_tensor_scan(flat(w.bb), e3, e4, 0.0, ALU.mult, ALU.add)
            dve.wait_ge(kv_ready, ci + 1)
            nc.vector.tensor_tensor_scan(flat(w.aa), e3, flat(w.kv), 0.0, ALU.mult, ALU.add).then_inc(sums_ready, 1)
            den = w.bb[:, :, 0:T]
            dve.wait_ge(e12_ready, ci + 1)
            dve.wait_ge(sums_ready, ci + 1)
            ch.link(nc.vector.tensor_tensor(den, den, w.e12[:, 0:w.S, :], ALU.mult))
            ch.link(nc.vector.tensor_tensor(den, den, w.e12[:, w.S:, :], ALU.add))

        def head_dve_inverse(dve, ch, w, ci):
            den = w.bb[:, :, 0:T]
            ch.link(nc.vector.reciprocal(den, den))

        def head_dve_out(dve, ch, w, b, ci):
            den, num = w.bb[:, :, 0:T], w.aa[:, :, 0:T]
            dve.wait_ge(num_ready, ci + 1)
            ch.link(nc.vector.scalar_tensor_tensor(num, num, tg[:, 0:1], den, ALU.mult, ALU.mult))
            v = xT[:, :, bass.ds(b * T, w.nb * T)]
            if w is pairs[1]:
                dve.wait_ge(xt0_loaded, 2 * 16)
                dve.wait_ge(x2_ready, 1)
                v = v.rearrange("p k (s t) -> p k s t", t=T)
                num = num.rearrange("p (k s) t -> p k s t", k=KH)
                nc.vector.tensor_tensor(v, num, v, ALU.add).then_inc(x2_ready, 1)
            elif w is one:
                dve.wait_ge(nat_ready, ci)
                if not (isinstance(ci, int) and ci == one.first_call):
                    dve.wait_ge(x2_stored, ci - 2)
                lone_wait(dve)
                nc.vector.tensor_tensor(w.x2, num, v, ALU.add).then_inc(x2_ready, 1)
            assert ch.n == HEAD_LINKS, ch.n

        def norm_dve_stats(dve, w, ci):
            dve.wait_ge(nat_ready, ci + 1)
            stats(norm_chain(dve, w, ci, w.norm2_step), lambda i: w.ps_nat[:, i, :], w, w.st2, w.mv2, w.ve2, var2_ready)

        def norm_dve(dve, w, ci):
            if w.nb == 1:
                dve.wait_ge(xnT_ready, ci)
            normalise(dve, lambda i: w.ps_nat[:, i, :], lambda i: w.xn2[:, i, :], w, w.mv2, w.rs2, rs2_ready, ci, xn2_ready)

        def across(w, a):
            return a.broadcast_to([P, w.nb, NE])

        def route_dve_logits(dve, ch, w, rc):
            dve.wait_ge(lg_ready, rc + 1)
            ch.link(nc.vector.reduce_max(w.top, w.ps_lg, AX))
            nc.vector.tensor_tensor(w.lg, w.ps_lg, across(w, w.top), ALU.subtract).then_inc(below_ready, 1)

        def route_dve(dve, ch, w, rc):
            nbs = range(w.nb)
            dve.wait_ge(exp_ready, rc + 1)
            lone_wait(dve)
            for i in nbs:
                last = nc.vector.max(w.e8[:, i, :], w.E[:, i, :])
            ch.link(last)
            ch.link(nc.vector.reduce_sum(w.s8, w.e8, AX))
            ch.link(nc.vector.tensor_scalar(w.tgt, w.e8[:, :, 0:1], tg[:, 2:3], None, ALU.mult))
            nc.vector.reciprocal(w.r8, w.s8)
            ch.link(nc.vector.scalar_tensor_tensor(w.tgt, w.e8[:, :, 7:8], tg[:, 3:4], w.tgt, ALU.mult, ALU.add))
            lone_wait(dve)
            for i in nbs:
                nc.vector.match_replace(w.left[:, i, :], w.e8[:, i, :], w.E[:, i, :], -1.0)
            ch.link(nc.vector.tensor_tensor(w.vn, w.E, across(w, w.r8), ALU.mult))
            nc.vector.tensor_tensor(w.eq, w.E, across(w, w.tgt), ALU.is_equal)
            ch.link(nc.vector.tensor_scalar(w.act, w.vn, par[:, 6:7], TAU, ALU.mult, ALU.is_ge))
            for i in nbs:
                nc.vector.tensor_tensor_scan(w.cs[:, i, :], ones32[:], w.eq[:, i, :], 0.0, ALU.mult, ALU.add)
            ch.link(nc.vector.scalar_tensor_tensor(w.act, w.left, 0.0, w.act, ALU.is_lt, ALU.mult))
            nc.vector.scalar_tensor_tensor(w.eq, w.cs, 1.0, w.eq, ALU.is_equal, ALU.mult)
            ch.link(nc.vector.reduce_max(w.any, w.act, AX))
            ch.link(nc.vector.tensor_tensor(w.eq, w.eq, across(w, w.any), ALU.is_gt))
            ch.link(nc.vector.tensor_tensor(w.act, w.act, w.eq, ALU.max))
            ch.link(nc.vector.tensor_tensor(w.wg, w.vn, w.act, ALU.mult))
            ch.link(nc.vector.reduce_sum(w.ws, w.wg, AX))
            ch.link(nc.vector.tensor_scalar(w.ws, w.ws, 1e-12, None, ALU.max))
            ch.link(nc.vector.reciprocal(w.rw, w.ws))
            if w.nb == 1:
                dve.wait_ge(cT_ready, rc)
            nc.vector.tensor_tensor(w.c, w.wg, across(w, w.rw), ALU.mult).then_inc(c_ready, 1)
            assert ch.n == ROUTE_LINKS, ch.n

        def unit_dve_prod(dve, n, s):
            dve.wait_ge(silu_ready, n + 1)
            nc.vector.tensor_tensor(hidden[:, s % 3, :], hidden[:, s % 3, :], ps_gu[:, s % 2, 1, :],
                                    ALU.mult).then_inc(prod_ready, 1)

        def unit_dve_h(dve, n, s, use):
            dve.wait_ge(prod_ready, n + 1 + CREDIT)
            dve.wait_ge(comb_loaded[s % 3], 32 * use)
            nc.vector.tensor_tensor(hidden[:, s % 3, :], hidden[:, s % 3, :], comb_of[:, s % 3, :],
                                    ALU.mult).then_inc(h_ready, 1)

        def evacuate(dve, g):
            dve.wait_ge(down_done, NJ * (g + 1) + CREDIT)
            if g:
                dve.wait_ge(x2_stored, BG * g)
            for m in range(KH):
                v = xT[:, m, bass.ts(g, GTOK)]
                nc.vector.scalar_tensor_tensor(v, ps_acc[:, m, :], tg[:, 1:2], v, ALU.mult, ALU.add).then_inc(evac_ready, 1)

        @block.vector
        def _(dve):
            dve.sem_inc(prod_ready, CREDIT)
            dve.sem_inc(h_ready, CREDIT)
            works = (*pairs, one)
            for w in works:
                nc.vector.memset(w.k[:, :, 0:1], NEG)
                nc.vector.memset(w.kv[:, :, 0:1], 0.0)
                nc.vector.memset(w.e34[:, :, 0:1], 0.0)
                nc.vector.memset(w.dec[:, :, 1:], 0.0)
                last = nc.vector.memset(w.dec[:, :, 0:1], 2 * NEG)
            last.then_inc(pads_set, 1)
            heads = [head_chain(dve, pairs[i], i) for i in range(2)]
            for i in range(2):
                dve.wait_ge(x0_loaded[i], 16)
                head_dve_stats(dve, pairs[i], PAIR * i, i)
            for i in range(2):
                head_dve_norm(dve, pairs[i], PAIR * i, i)
            for i in range(2):
                dve.wait_ge(dec_ready, i + 1)
                head_dve_max(dve, heads[i], pairs[i], i)
                head_dve_ends(dve, pairs[i], i)
            dve.wait_ge(gates_ready, 1)
            nc.vector.tensor_scalar(tg[:, 1:2], tg[:, 1:2], 1.0 / WSCALE, None, ALU.mult)
            nc.vector.tensor_scalar(tg[:, 2:3], par[:, 6:7], 0.0, None, ALU.is_ge)
            nc.vector.tensor_scalar(tg[:, 3:4], par[:, 6:7], 0.0, None, ALU.is_lt)
            nc.vector.scalar_tensor_tensor(gate_lo[:], gate_w[:], WSCALE, gate_hi[:], ALU.mult,
                                           ALU.subtract).then_inc(gate_split, 1)
            dve.wait_ge(gate_split, 1)
            for i in range(2):
                head_dve_sums(dve, heads[i], pairs[i], i)
            head_dve_inverse(dve, heads[0], pairs[0], 0)
            head_dve_out(dve, heads[0], pairs[0], 0, 0)
            head_dve_inverse(dve, heads[1], pairs[1], 1)
            head_dve_out(dve, heads[1], pairs[1], PAIR, 1)
            for i in range(2):
                norm_dve_stats(dve, pairs[i], i)
            for i in range(2):
                norm_dve(dve, pairs[i], i)
            ch = head_chain(dve, one, 2)
            dve.wait_ge(xrest_loaded, (2 * NG - 1) * 16)
            head_dve_stats(dve, one, BG, 2)
            head_dve_norm(dve, one, BG, 2)
            head_dve_stats(dve, one, BG + 1, 3)
            dve.wait_ge(dec_ready, 3)
            head_dve_max(dve, ch, one, 2)
            cg = route_chain(dve, group, 0)
            route_dve_logits(dve, cg, group, 0)
            head_dve_ends(dve, one, 2)
            route_dve(dve, cg, group, 0)
            unit_dve_prod(dve, 0, 0)
            head_dve_sums(dve, ch, one, 2)
            unit_dve_prod(dve, 1, 1)
            head_dve_inverse(dve, ch, one, 2)
            unit_dve_prod(dve, 2, 2)
            head_dve_out(dve, ch, one, BG, 2)
            unit_dve_h(dve, 0, 0, 1)
            unit_dve_h(dve, 1, 1, 1)
            norm_dve_stats(dve, one, 2)
            head_dve_norm(dve, one, BG + 1, 3)
            norm_dve(dve, one, 2)

            def step(t, prep, now, then):
                head = head_chain(dve, one, t + 3)
                head.n = 1
                route = route_chain(dve, single, t + 1)
                for s in range(UPS):
                    n = UPS * t + s
                    if s == 4 and then:
                        norm_dve_stats(dve, one, t + 3)
                    if s == 4 and then == 2:
                        head_dve_norm(dve, one, t + 6, t + 4)
                    if unit(t, s, 2):
                        if not (s == 0 and is_(t, 0)):
                            unit_dve_prod(dve, n + 2, s + 2)
                        unit_dve_h(dve, n + 2, s + 2, 2 * t + (s + 2) // 3 + 1)
                    if s == UPS - 1 and closes(t):
                        evacuate(dve, t // SPG)
                    if s == 0 and is_(t, 0):
                        head_dve_max(dve, head_chain(dve, one, 3), one, 3)
                    if s == (1 if is_(t, 0) else 0) and now:
                        route_dve_logits(dve, route, single, t + 1)
                    if s == 0 and now == 2:
                        head_dve_ends(dve, one, t + 3)
                    if s == 0 and then == 2:
                        head_dve_stats(dve, one, t + 6, t + 4)
                    if s == 1 and now:
                        route_dve(dve, route, single, t + 1)
                    if s == 2 and now == 2:
                        head_dve_sums(dve, head, one, t + 3)
                        head_dve_inverse(dve, head, one, t + 3)
                        head_dve_out(dve, head, one, t + 5, t + 3)
                    if s == 4 and then:
                        norm_dve(dve, one, t + 3)
                    if s == 5 and then == 2:
                        head_dve_max(dve, head_chain(dve, one, t + 4), one, t + 4)

            run_steps(dve, step)

        def head_pe_keys(pe, w, ci):
            pe.wait_ge(xn1_ready, ci + 1)
            for i in range(w.nb):
                for kh in range(KH):
                    last = nc.tensor.transpose(w.ps_kT[:, kh * w.nb + i, :], w.xn[:, i, kh * P:(kh + 1) * P], ident[:])
            last.then_inc(kT_ready, 1)

        def head_pe_natural(pe, w, b, ci):
            pe.wait_ge(x2_ready, ci + 1)
            if w.nb == 1:
                pe.wait_ge(xf_copied, ci)
            for i in range(w.nb):
                for kh in range(KH):
                    src = xT[:, kh, (b + i) * T:(b + i + 1) * T] if w.x2 is None else w.x2[:, kh, :]
                    last = nc.tensor.transpose(w.ps_nat[:, i, kh * P:(kh + 1) * P], src, ident[:])
            last.then_inc(nat_ready, 1)

        def tail_pe_normalised(pe, w, ci):
            pe.wait_ge(xn2_ready, ci + 1)
            for i in range(w.nb):
                for kh in range(KH):
                    last = nc.tensor.transpose(w.ps_xnT[:, kh * w.nb + i, :], w.xn2[:, i, kh * P:(kh + 1) * P], ident[:])
            last.then_inc(xnT_ready, 1)

        def route_pe_logits(pe, r, b, rc):
            pe.wait_ge(xl_ready, rc + 2)
            if r.nb == 1:
                pe.wait_ge(comb_ready, rc)
            for i in range(r.nb):
                tok = bass.ds((b + i) * T, T)
                for kh in range(KH):
                    for p, (xx, gw) in enumerate(((xn_hi, gate_hi), (xn_lo, gate_hi), (xn_hi, gate_lo))):
                        last = nc.tensor.matmul(r.ps_lg[:, i, :], xx[:, kh, tok], gw[:, kh, :],
                                                start=(kh == 0 and p == 0), stop=(kh == KH - 1 and p == 2))
            last.then_inc(lg_ready, 1)

        def route_pe_comb(pe, r, rc):
            pe.wait_ge(c_ready, rc + 1)
            lone_wait(pe)
            for i in range(r.nb):
                last = nc.tensor.transpose(r.ps_cT[:, i, :], r.c[:, i, :], ident[:])
            last.then_inc(cT_ready, 1)

        def gate_up(pe, n, s, j, g):
            pe.wait_ge(prod_ready, n - 1 + CREDIT)
            for gu in range(2):
                for kh in range(KH):
                    col = bass.ds(j * WT_COLS + (kh * 2 + gu) * P, P)
                    tok = bass.ds(g * GTOK, GTOK)
                    for i, (w, xx) in enumerate(((w_hi, xn_hi), (w_hi, xn_lo), (w_lo, xn_hi))):
                        last = nc.tensor.matmul(ps_gu[:, s % 2, gu, :], w[:, col], xx[:, kh, tok],
                                                start=(kh == 0 and i == 0), stop=(kh == KH - 1 and i == 2))
            last.then_inc(gu_done, 1)

        def down(pe, n, s, j, first_of_group, last_of_group):
            pe.wait_ge(hl_ready, n + 1 + CREDIT)
            for m in range(KH):
                col = bass.ds(j * WT_COLS + 2 * KH * P + m * P, P)
                for i, (w, h) in enumerate(((w_hi, h_hi), (w_hi, h_lo), (w_lo, h_hi))):
                    last = nc.tensor.matmul(ps_acc[:, m, :], w[:, col], h[:, s % 3, :],
                                            start=first_of_group and i == 0, stop=last_of_group and i == 2,
                                            skip_group_check=True)
            last.then_inc(down_done, 1)

        @block.tensor
        def _(pe):
            pe.sem_inc(down_done, CREDIT)
            pe.wait_ge(consts_ready, 1)
            for i in range(2):
                head_pe_keys(pe, pairs[i], i)
            for i in range(2):
                head_pe_natural(pe, pairs[i], PAIR * i, i)
            for i in range(2):
                tail_pe_normalised(pe, pairs[i], i)
            head_pe_keys(pe, one, 2)
            pe.wait_ge(gate_split, 1)
            route_pe_logits(pe, group, 0, 0)
            pe.wait_ge(w_ready, 2)
            for n in range(2):
                gate_up(pe, n, n, n, 0)
            route_pe_comb(pe, group, 0)

            def step(t, prep, now, then):
                for s in range(UPS):
                    n = UPS * t + s
                    begun = unit(t, s, 2)
                    if begun:
                        t2, s2 = begun
                        if then and s == 4:
                            pe.wait_ge(xl_ready, t + 3)
                        if prep or (is_(t, SPG - 1) and s < UPS - 2):
                            pe.wait_ge(w_ready, n + 3)
                        if not (s in (1, 2) and is_(t, 0)):
                            gate_up(pe, n + 2, s, UPS * (t2 % SPG) + s2, t2 // SPG)
                    if s == 0 and is_(t, 0):
                        pe.wait_ge(w_ready, 5)
                        gate_up(pe, 3, 1, 3, 0)
                        gate_up(pe, 4, 0, 4, 0)
                        head_pe_natural(pe, one, BG, 2)
                    if s == (4 if is_(t, 0) else 3) and now:
                        route_pe_comb(pe, single, t + 1)
                    if s == 2 and is_(t, 0):
                        route_pe_logits(pe, single, BG, 1)
                    first = opens(t) and s == 0
                    if first and t > 0:
                        pe.wait_ge(evac_ready, KH * (t // SPG))
                    down(pe, n, s, UPS * (t % SPG) + s, first, closes(t) and s == UPS - 1)
                    if s == 0 and is_(t, 0):
                        tail_pe_normalised(pe, one, 2)
                        head_pe_keys(pe, one, 3)
                    if s == 0 and now and not is_(t, 0):
                        route_pe_logits(pe, single, t + BG, t + 1)
                    if s == 4 and then:
                        head_pe_natural(pe, one, t + 5, t + 3)
                    if s == 5 and then:
                        tail_pe_normalised(pe, one, t + 3)
                    if s == 5 and then == 2:
                        head_pe_keys(pe, one, t + 4)

            run_steps(pe, step)


def kernel(x, ctx_2048, g_xattn, g_ffn, L0_xattn_time_decay, L0_xattn_time_first, L0_ffn_gate_weight,
           L0_ffn_gate_up_proj, L0_ffn_down_proj, L0_ffn_layer_alpha):
    import numpy as np
    import concourse.bacc as bacc
    from concourse.bass_utils import run_bass_kernel_spmd

    def transposed(a):
        a = np.asarray(a).reshape(NG, GTOK, KH, P)
        return np.ascontiguousarray(a.transpose(0, 3, 2, 1))

    def per_channel(v):
        return np.asarray(v).reshape(KH, P).T

    def everywhere(v):
        return np.broadcast_to(np.asarray(v).reshape(1, 1), (P, 1))

    params = np.ascontiguousarray(np.concatenate(
        [per_channel(L0_xattn_time_decay), per_channel(L0_xattn_time_first), everywhere(g_xattn), everywhere(g_ffn),
         everywhere(L0_ffn_layer_alpha), everywhere(L0_ffn_layer_alpha)], axis=1))
    gate_up = np.asarray(L0_ffn_gate_up_proj).reshape(NE, 2, INTER, KH, P)
    gate_up = gate_up.transpose(1, 0, 2, 3, 4).reshape(2, NJ, P, KH, P)
    gate_up = gate_up.transpose(1, 4, 3, 0, 2).reshape(NJ, P, 2 * KH * P)
    down = np.asarray(L0_ffn_down_proj).transpose(0, 2, 1).reshape(NJ, P, C)
    weights = np.ascontiguousarray(np.concatenate([gate_up, down], axis=2))
    gate_wt = np.ascontiguousarray(np.asarray(L0_ffn_gate_weight).reshape(NE, KH, P).transpose(2, 1, 0))

    arrays = {"in_x": np.ascontiguousarray(x), "in_xt": transposed(x), "in_ctx": transposed(ctx_2048),
              "in_params": params, "in_gate": gate_wt, "in_weights": weights}
    nc = bacc.Bacc("TRN2", target_bir_lowering=False, num_devices=1)
    args = [nc.dram_tensor(name, a.shape, mybir.dt.from_np(a.dtype), kind="ExternalInput").ap()
            for name, a in arrays.items()]
    args.append(nc.dram_tensor("out_y", (NG, P, KH, GTOK), F32, kind="ExternalOutput").ap())
    args.append(nc.dram_tensor("comb_dram", (NE, NTOK), F32, kind="Internal").ap())
    rwkv_moe_kernel(nc, *args)
    r = run_bass_kernel_spmd(nc, [arrays], core_ids=[0])
    y = r.results[0]["out_y"]
    return y.transpose(0, 3, 2, 1).reshape(B, T, C)
```
